# Optimizing a Trainium2 kernel written in Bass

```python
import numpy as np
import jax
import jax.numpy as jnp

def _softmax(x, axis=-1):
    return jax.nn.softmax(x, axis=axis)

def _gelu(x):
    return jax.nn.gelu(x, approximate=True)

def _silu(x):
    return jax.nn.silu(x)

def _sigmoid(x):
    return jax.nn.sigmoid(x)

def _layernorm(x, axis=-1, eps=1e-05):
    m = jnp.mean(x, axis=axis, keepdims=True)
    v = jnp.var(x, axis=axis, keepdims=True)
    return (x - m) / jnp.sqrt(v + eps)

def _scatter_add(tgt, idx, src, axis=0):
    return tgt.at[idx].add(src)

def _segment_sum(src, seg, n):
    return jax.ops.segment_sum(src, seg, n)
kernel_name = 'mk_gnn_resnorm_d4_gnn_r16_6fe312'

def setup_inputs(seed: int=0):
    np.random.seed(seed)
    _w = jnp.asarray

    def _rec_inputs():
        import jax
        import jax.numpy as jnp
        _gk = jax.random.key(seed)
        x = -0.0003713 + 1 * jax.random.normal(jax.random.fold_in(_gk, 1), (6250, 128), jnp.float32)
        _s = jax.random.randint(jax.random.fold_in(_gk, 2), (50000,), 0, 6250, jnp.int32)
        _d = jax.random.randint(jax.random.fold_in(_gk, 3), (50000,), 0, 6250, jnp.int32)
        _loop = jnp.arange(6250, dtype=jnp.int32)
        src = jnp.concatenate([_s, _d, _loop])
        dst = jnp.concatenate([_d, _s, _loop])
        _o = jnp.argsort(dst, stable=True)
        src = src[_o]
        dst = dst[_o]
        edge_attr_64 = 0.000135552 + 1.00015 * jax.random.normal(jax.random.fold_in(_gk, 12), (106250, 64), jnp.float32)
        return (x, src, dst, edge_attr_64)
    x, src, dst, edge_attr_64 = _rec_inputs()

    def _L0_gnn_setup():
        import jax, jax.numpy as jnp
        import numpy as np
        EPS = 0.0
        key = jax.random.key(seed)
        k_x, k_e, k_w1, k_w2 = jax.random.split(key, 4)
        N, E, D = (6250, 625000, 128)
        x = jax.random.normal(k_x, (N, D), dtype=jnp.float32)
        edge_index = jax.random.randint(k_e, (2, E), 0, N, dtype=jnp.int32)
        s = 1.0 / np.sqrt(D)
        W1 = jax.random.normal(k_w1, (D, D), dtype=jnp.float32) * s
        b1 = jnp.zeros((D,), dtype=jnp.float32)
        W2 = jax.random.normal(k_w2, (D, D), dtype=jnp.float32) * s
        b2 = jnp.zeros((D,), dtype=jnp.float32)
        return {'x': x, 'edge_index': edge_index, 'W1': W1, 'b1': b1, 'W2': W2, 'b2': b2}
    _L0_gnn_all = _L0_gnn_setup()
    _L0_gnn_in = {k: v for k, v in _L0_gnn_all.items() if k in ('W1', 'b1', 'W2', 'b2')}
    del _L0_gnn_all

    def _L1_gnn_setup():
        import jax, jax.numpy as jnp
        import numpy as np
        N = 3125
        E = 50000
        F_IN = 128
        HID = 128
        OUT = 128

        def _lin_init(key, fan_in, fan_out):
            s = 1.0 / np.sqrt(fan_in)
            kw, kb = jax.random.split(key)
            W = jax.random.uniform(kw, (fan_in, fan_out), minval=-s, maxval=s, dtype=jnp.float32)
            b = jax.random.uniform(kb, (fan_out,), minval=-s, maxval=s, dtype=jnp.float32)
            return (W, b)
        key = jax.random.key(seed)
        kx, ke, k1, k2, k3, k4 = jax.random.split(key, 6)
        x = jax.random.normal(kx, (N, F_IN), dtype=jnp.float32)
        edge_index = jax.random.randint(ke, (2, E), 0, N, dtype=jnp.int32)
        W1, b1 = _lin_init(k1, F_IN, HID)
        W2, b2 = _lin_init(k2, HID, HID)
        W3, b3 = _lin_init(k3, HID, HID)
        W4, b4 = _lin_init(k4, HID, OUT)
        return {'x': x, 'edge_index': edge_index, 'W1': W1, 'b1': b1, 'W2': W2, 'b2': b2, 'W3': W3, 'b3': b3, 'W4': W4, 'b4': b4}
    _L1_gnn_all = _L1_gnn_setup()
    _L1_gnn_in = {k: v for k, v in _L1_gnn_all.items() if k in ('W1', 'b1', 'W2', 'b2', 'W3', 'b3', 'W4', 'b4')}
    del _L1_gnn_all

    def _L2_gnn_setup():
        import jax, jax.numpy as jnp
        import numpy as np
        N_NODES = 3125
        N_EDGES = 50000
        NODE_DIM = 128
        EDGE_DIM = 64
        key = jax.random.key(seed)
        ks = jax.random.split(key, 9)
        src = jax.random.randint(ks[0], (N_EDGES,), 0, N_NODES)
        dst = jax.random.randint(ks[1], (N_EDGES,), 0, N_NODES)
        nfeat = jax.random.normal(ks[2], (N_NODES, NODE_DIM), dtype=jnp.float32)
        efeat = jax.random.normal(ks[3], (N_EDGES, EDGE_DIM), dtype=jnp.float32)
        Wn = jax.random.normal(ks[4], (NODE_DIM, NODE_DIM), dtype=jnp.float32) * NODE_DIM ** (-0.5)
        bn = jax.random.normal(ks[5], (NODE_DIM,), dtype=jnp.float32) * 0.02
        We = jax.random.normal(ks[6], (EDGE_DIM, NODE_DIM), dtype=jnp.float32) * EDGE_DIM ** (-0.5)
        be = jax.random.normal(ks[7], (NODE_DIM,), dtype=jnp.float32) * 0.02
        resid = jax.random.normal(ks[8], (1, NODE_DIM), dtype=jnp.float32) * 0.02
        return {'src': src, 'dst': dst, 'nfeat': nfeat, 'efeat': efeat, 'Wn': Wn, 'bn': bn, 'We': We, 'be': be, 'resid': resid}
    _L2_gnn_all = _L2_gnn_setup()
    _L2_gnn_in = {k: v for k, v in _L2_gnn_all.items() if k in ('Wn', 'bn', 'We', 'be', 'resid')}
    del _L2_gnn_all

    def _L3_gnn_setup():
        import jax, jax.numpy as jnp
        import numpy as np
        N_NODES = 3125
        N_EDGES = 50000
        D_IN = 128
        D_HID = 128

        def _sage_conv(x, src, dst, W_l, b_l, W_r, num_nodes):
            msgs = x[src]
            agg = jax.ops.segment_sum(msgs, dst, num_segments=num_nodes)
            cnt = jax.ops.segment_sum(jnp.ones((dst.shape[0], 1), x.dtype), dst, num_segments=num_nodes)
            agg = agg / jnp.maximum(cnt, 1.0)
            return agg @ W_l.T + b_l + x @ W_r.T
        key = jax.random.key(seed)
        ks = jax.random.split(key, 8)
        x = jax.random.normal(ks[0], (N_NODES, D_IN), dtype=jnp.float32)
        edge_index = jax.random.randint(ks[1], (2, N_EDGES), 0, N_NODES, dtype=jnp.int64)
        s0 = 1.0 / np.sqrt(D_IN)
        s1 = 1.0 / np.sqrt(D_HID)
        return {'x': x, 'edge_index': edge_index, 'W_l0': jax.random.uniform(ks[2], (D_HID, D_IN), jnp.float32, -s0, s0), 'b_l0': jnp.zeros((D_HID,), jnp.float32), 'W_r0': jax.random.uniform(ks[3], (D_HID, D_IN), jnp.float32, -s0, s0), 'W_l1': jax.random.uniform(ks[4], (D_HID, D_HID), jnp.float32, -s1, s1), 'b_l1': jnp.zeros((D_HID,), jnp.float32), 'W_r1': jax.random.uniform(ks[5], (D_HID, D_HID), jnp.float32, -s1, s1)}
    _L3_gnn_all = _L3_gnn_setup()
    _L3_gnn_in = {k: v for k, v in _L3_gnn_all.items() if k in ('W_l0', 'b_l0', 'W_r0', 'W_l1', 'b_l1', 'W_r1')}
    del _L3_gnn_all
    return {'x': x, 'src': src, 'dst': dst, 'edge_attr_64': edge_attr_64, 'L0_gnn_W1': _L0_gnn_in['W1'], 'L0_gnn_b1': _L0_gnn_in['b1'], 'L0_gnn_W2': _L0_gnn_in['W2'], 'L0_gnn_b2': _L0_gnn_in['b2'], 'L1_gnn_W1': _L1_gnn_in['W1'], 'L1_gnn_b1': _L1_gnn_in['b1'], 'L1_gnn_W2': _L1_gnn_in['W2'], 'L1_gnn_b2': _L1_gnn_in['b2'], 'L1_gnn_W3': _L1_gnn_in['W3'], 'L1_gnn_b3': _L1_gnn_in['b3'], 'L1_gnn_W4': _L1_gnn_in['W4'], 'L1_gnn_b4': _L1_gnn_in['b4'], 'L2_gnn_Wn': _L2_gnn_in['Wn'], 'L2_gnn_bn': _L2_gnn_in['bn'], 'L2_gnn_We': _L2_gnn_in['We'], 'L2_gnn_be': _L2_gnn_in['be'], 'L2_gnn_resid': _L2_gnn_in['resid'], 'L3_gnn_W_l0': _L3_gnn_in['W_l0'], 'L3_gnn_b_l0': _L3_gnn_in['b_l0'], 'L3_gnn_W_r0': _L3_gnn_in['W_r0'], 'L3_gnn_W_l1': _L3_gnn_in['W_l1'], 'L3_gnn_b_l1': _L3_gnn_in['b_l1'], 'L3_gnn_W_r1': _L3_gnn_in['W_r1']}

def reference(x, src, dst, edge_attr_64, L0_gnn_W1, L0_gnn_b1, L0_gnn_W2, L0_gnn_b2, L1_gnn_W1, L1_gnn_b1, L1_gnn_W2, L1_gnn_b2, L1_gnn_W3, L1_gnn_b3, L1_gnn_W4, L1_gnn_b4, L2_gnn_Wn, L2_gnn_bn, L2_gnn_We, L2_gnn_be, L2_gnn_resid, L3_gnn_W_l0, L3_gnn_b_l0, L3_gnn_W_r0, L3_gnn_W_l1, L3_gnn_b_l1, L3_gnn_W_r1):
    import jax
    import jax.numpy as jnp

    def _L0_gnn_ref(x, edge_index, W1, b1, W2, b2):
        import jax, jax.numpy as jnp
        import numpy as np
        EPS = 0.0
        src = edge_index[0]
        dst = edge_index[1]
        agg = jax.ops.segment_sum(x[src], dst, num_segments=x.shape[0])
        h = (1.0 + EPS) * x + agg
        h = jax.nn.relu(h @ W1.T + b1)
        h = h @ W2.T + b2
        return jax.nn.relu(h)

    def _L1_gnn_ref(x, edge_index, W1, b1, W2, b2, W3, b3, W4, b4):
        import jax, jax.numpy as jnp
        import numpy as np
        N = 3125
        E = 50000
        F_IN = 128
        HID = 128
        OUT = 128

        def _lin_init(key, fan_in, fan_out):
            s = 1.0 / np.sqrt(fan_in)
            kw, kb = jax.random.split(key)
            W = jax.random.uniform(kw, (fan_in, fan_out), minval=-s, maxval=s, dtype=jnp.float32)
            b = jax.random.uniform(kb, (fan_out,), minval=-s, maxval=s, dtype=jnp.float32)
            return (W, b)
        n = x.shape[0]
        loop = jnp.arange(n, dtype=edge_index.dtype)
        src = jnp.concatenate([edge_index[0], loop])
        dst = jnp.concatenate([edge_index[1], loop])
        deg = jax.ops.segment_sum(jnp.ones(src.shape[0], dtype=x.dtype), dst, num_segments=n)
        dinv = jnp.where(deg > 0, jax.lax.rsqrt(deg), 0.0)
        norm = dinv[src] * dinv[dst]

        def gcn_conv(h, W, b):
            h = h @ W
            msg = h[src] * norm[:, None]
            agg = jax.ops.segment_sum(msg, dst, num_segments=n)
            return agg + b
        h = jax.nn.relu(gcn_conv(x, W1, b1))
        h = jax.nn.relu(gcn_conv(h, W2, b2))
        h = jax.nn.relu(gcn_conv(h, W3, b3))
        return gcn_conv(h, W4, b4)

    def _L2_gnn_ref(src, dst, nfeat, efeat, Wn, bn, We, be, resid):
        import jax, jax.numpy as jnp
        import numpy as np
        N_NODES = 3125
        N_EDGES = 50000
        NODE_DIM = 128
        EDGE_DIM = 64
        N = nfeat.shape[0]
        in_deg = jax.ops.segment_sum(jnp.ones(src.shape[0], dtype=nfeat.dtype), dst, num_segments=N)
        degs = in_deg + 1.0
        norm = degs ** (-0.5)
        edge_norm = (norm[src] * norm[dst])[:, None]
        h = nfeat @ Wn + bn
        e = efeat @ We + be
        msg = edge_norm * (h[src] + e)
        agg = jax.ops.segment_sum(msg, dst, num_segments=N)
        residual = (h + resid) / degs[:, None]
        return agg + residual

    def _L3_gnn_ref(x, edge_index, W_l0, b_l0, W_r0, W_l1, b_l1, W_r1):
        import jax, jax.numpy as jnp
        import numpy as np
        N_NODES = 3125
        N_EDGES = 50000
        D_IN = 128
        D_HID = 128

        def _sage_conv(x, src, dst, W_l, b_l, W_r, num_nodes):
            msgs = x[src]
            agg = jax.ops.segment_sum(msgs, dst, num_segments=num_nodes)
            cnt = jax.ops.segment_sum(jnp.ones((dst.shape[0], 1), x.dtype), dst, num_segments=num_nodes)
            agg = agg / jnp.maximum(cnt, 1.0)
            return agg @ W_l.T + b_l + x @ W_r.T
        src, dst = (edge_index[0], edge_index[1])
        n = x.shape[0]
        h = _sage_conv(x, src, dst, W_l0, b_l0, W_r0, n)
        h = jax.nn.relu(h)
        out = _sage_conv(h, src, dst, W_l1, b_l1, W_r1, n)
        return out
    edge_index = jnp.stack([src, dst])
    x = _layernorm(x + _L0_gnn_ref(x, edge_index, L0_gnn_W1, L0_gnn_b1, L0_gnn_W2, L0_gnn_b2), axis=-1)
    x = _layernorm(x + _L1_gnn_ref(x, edge_index, L1_gnn_W1, L1_gnn_b1, L1_gnn_W2, L1_gnn_b2, L1_gnn_W3, L1_gnn_b3, L1_gnn_W4, L1_gnn_b4), axis=-1)
    x = _layernorm(x + _L2_gnn_ref(src, dst, x, edge_attr_64, L2_gnn_Wn, L2_gnn_bn, L2_gnn_We, L2_gnn_be, L2_gnn_resid), axis=-1)
    x = _layernorm(x + _L3_gnn_ref(x, edge_index, L3_gnn_W_l0, L3_gnn_b_l0, L3_gnn_W_r0, L3_gnn_W_l1, L3_gnn_b_l1, L3_gnn_W_r1), axis=-1)
    return x

_drawn_inputs = setup_inputs


def setup_inputs(seed=0):
    import zlib

    import numpy as np

    out = dict(_drawn_inputs(seed))
    spreads = {'L0_gnn_b1': (0.0, 0.329),
     'L0_gnn_b2': (0.0, 0.1),
     'L3_gnn_b_l0': (0.0, 0.1),
     'L3_gnn_b_l1': (0.0, 0.1)}
    factors = {'L1_gnn_W1': 5.358,
     'L1_gnn_b1': 8.0,
     'L1_gnn_W2': 3.099,
     'L1_gnn_b2': 5.254,
     'L1_gnn_W3': 2.693,
     'L2_gnn_be': 3.104,
     'L2_gnn_resid': 56.09,
     'L1_gnn_b3': 3.206,
     'L2_gnn_bn': 3.001}
    for name, (base, spread) in spreads.items():
        noise = np.random.default_rng([zlib.crc32(name.encode()), seed]).standard_normal(out[name].shape)
        drawn = base * np.exp(spread * noise) if base else spread * noise
        out[name] = jnp.asarray(drawn.astype(out[name].dtype))
    for name, factor in factors.items():
        out[name] = (out[name] * factor).astype(out[name].dtype)
    return out
```

```python
import concourse.bass as bass
from concourse import mybir
from contextlib import ExitStack

P = 128


def build(nc, a, out):
    fp32 = mybir.dt.float32
    i32 = mybir.dt.int32
    ALU = mybir.AluOpType
    ACT = mybir.ActivationFunctionType
    AX = mybir.AxisListType.X
    ds = bass.ds

    N, D = a["x"].shape
    E, DE = a["edge_attr_64"].shape
    NB = -(-N // P)
    NP = NB * P
    NTAIL = N - (NB - 1) * P
    J = 17
    GE = P * J
    NG = -(-E // GE)
    PTAIL = (E - (NG - 1) * GE) // J
    assert PTAIL * J == E - (NG - 1) * GE
    NT = NG * J
    PADNODE = NP - 1
    QB = 7
    NQ = NB // QB
    QN = QB * P
    UN = QN // 2
    EPS = 1e-5
    FAR = 1.0e6

    Hd = nc.dram_tensor("h_rows", (NP, D), fp32).ap()
    Gd = nc.dram_tensor("sum_rows", (NP, D), fp32).ap()
    Ed = nc.dram_tensor("attr_rows", (NP, D), fp32).ap()
    dinv_d = nc.dram_tensor("dinv_vec", (NP,), fp32).ap()
    rc_d = nc.dram_tensor("rc_vec", (NP,), fp32).ap()

    PASSES = ["cnt", "attr"] + list(range(8))
    SELF = [0, 1, 2, 3, 4]

    with ExitStack() as ctx:
        def sb(name, shape, dt=fp32):
            return ctx.enter_context(nc.sbuf_tensor(name, shape, dt))

        def sem(name):
            return ctx.enter_context(nc.semaphore(name))

        XN = sb("XN", [P, NP])
        HN = sb("HN", [P, NP])
        HR = sb("HR", [P, NP])
        AGN = sb("AGN", [P, NP])
        AT = sb("AT", [P, NP])
        TB = sb("TB", [P, NP])
        RB = sb("RB", [P, NP])
        T1 = sb("T1", [P, QN])
        ST = sb("ST", [P, QB, 6])
        MV = sb("MV", [P, QB, 2])
        VE = sb("VE", [P, QB])
        SD = sb("SD", [P, QB])
        RS = sb("RS", [P, QB])
        srcI = sb("srcI", [P, NT], i32)
        dstI = sb("dstI", [P, NT], i32)
        dstF = sb("dstF", [P, NT])
        ident = sb("ident", [P, P])
        ones = sb("ones", [P, P])
        zeros = sb("zeros", [P, P])
        low = sb("low", [P, P])
        WR = sb("WR", [P, 6, P])
        WT = sb("WT", [P, 6, P])
        WN = sb("WN", [P, 5, P])
        We2 = sb("We2", [P, P])
        BC = sb("BC", [P, 4])
        BR = sb("BR", [P, 7, P])
        CN = sb("CN", [P, NB])
        dinv = sb("dinv", [P, NB])
        rc = sb("rc", [P, NB])
        idg = sb("idg", [P, NB])
        c1 = sb("c1", [P, NB])
        c2 = sb("c2", [P, NB])
        SQ = sb("SQ", [P, NB])
        si = sb("si", [P, 1], i32)
        di = sb("di", [P, 1], i32)
        xi = sb("xi", [P, 1], i32)
        Dg = sb("Dg", [P, P])
        M = sb("M", [P, P])
        ML = sb("ML", [P, P])
        cl = sb("cl", [P, 1])
        far = sb("far", [P, 1])
        msg = sb("msg", [P, P])
        old = sb("old", [P, P])
        new = sb("new", [P, P])
        at = sb("at", [P, P])

        PS = ctx.enter_context(nc.psum_tensor("PS", [P, 4096], fp32))
        X, Y, Z = PS[:, 0:1024], PS[:, 1024:2048], PS[:, 2048:3072]
        PB, PC = PS[:, 3072:3072 + P], PS[:, 3584:3584 + P]

        s_w = sem("weights_loaded")
        s_cst = sem("constants_ready")
        s_idx = sem("indices_loaded")
        s_pad = sem("pads_set")
        s_dst = sem("dst_float")
        s_wt = sem("weights_transposed")
        s_wc = sem("weights_copied")
        s_x = sem("x_loaded")
        s_tab = {p: sem(f"tables_{p}") for p in PASSES}
        s_stage = {p: sem(f"staged_{p}") for p in PASSES}
        s_g = {p: sem(f"gathered_{p}") for p in PASSES}
        s_old = {p: sem(f"old_{p}") for p in PASSES}
        s_bc = {p: sem(f"dst_row_{p}") for p in PASSES}
        s_m = {p: sem(f"match_{p}") for p in PASSES}
        s_cmb = {p: sem(f"combined_{p}") for p in PASSES}
        s_new = {p: sem(f"new_{p}") for p in PASSES}
        s_sc = {p: sem(f"scattered_{p}") for p in PASSES}
        s_attr = sem("attr_tile")
        s_held = sem("held")
        s_scrap = sem("scrap")
        s_cn = sem("cnt_loaded")
        s_sq = sem("cnt_plus_one")
        s_sr = sem("cnt_root")
        s_deg = sem("degree_factors")
        s_dv = sem("factors_stored")
        s_rb = sem("factor_row_loaded")
        s_agn = sem("sums_loaded")
        s_ax = sem("sums_transposed")
        s_axf = sem("sums_transposed_free")
        s_at = sem("AT_ready")
        s_ea = sem("EA_ready")
        s_xf, s_xfree = sem("X_full"), sem("X_free")
        s_yf, s_yfree = sem("Y_full"), sem("Y_free")
        s_zf, s_zfree = sem("Z_full"), sem("Z_free")
        s_tb = sem("TB_ready")
        s_var = sem("variance")
        s_sd = sem("deviation")
        s_xn = sem("XN_ready")
        s_h = sem("H_ready")
        s_out = sem("stored")

        XU = dict(zip(range(9), [0, 7, 14, 14, 14, 14, 14, 14, 14]))
        YU = {0: 0, 1: 7, 2: 14, 3: 21, 4: 28, 5: 42, 6: 49, 7: 56}
        ZU = {4: 0, 5: 7, 6: 14}
        TU = {0: 0, 1: 7, 2: 14, 3: 21, 4: 28, 5: 35, 6: 42}
        LU = {0: 0, 4: 7, 5: 14, 7: 21}
        def agu(p):
            return 7 * p + (7 if p >= 4 else 0)

        block = ctx.enter_context(nc.Block())

        def tiles(eng, body):
            with eng.Fori(0, NG - 1) as g:
                with eng.Fori(0, J) as j:
                    body(g, j, g * J + j, P)
            with eng.Fori(0, J) as j:
                body(NG - 1, j, (NG - 1) * J + j, PTAIL)

        def rows(t):
            return t.rearrange("(b p) f -> p b f", p=P)

        def blk(t):
            return t[:, :].rearrange("p (b f) -> p b f", f=P)

        @block.sync
        def _(sp):
            for k, w in enumerate(["L0_gnn_W1", "L0_gnn_W2", "L3_gnn_W_l0", "L3_gnn_W_r0", "L3_gnn_W_l1", "L3_gnn_W_r1"]):
                sp.dma_start(WR[:, k, :], a[w][:, :]).then_inc(s_w, 16)
            for k, w in enumerate(["L1_gnn_W1", "L1_gnn_W2", "L1_gnn_W3", "L1_gnn_W4", "L2_gnn_Wn"]):
                sp.dma_start(WN[:, k, :], a[w][:, :]).then_inc(s_w, 16)
            for k in range(2):
                sp.dma_start(We2[DE * k:DE * k + DE, :], a["L2_gnn_We"][:, :]).then_inc(s_w, 16)
            with nc.allow_non_contiguous_dma(reason="a bias of 128 words on partitions"):
                for k, b in enumerate(["L0_gnn_b1", "L1_gnn_b1", "L1_gnn_b2", "L1_gnn_b3"]):
                    sp.dma_start(BC[:, k:k + 1], a[b].rearrange("(p o) -> p o", o=1)).then_inc(s_w, 16)
            for k, b in enumerate(["L0_gnn_b2", "L1_gnn_b4", "L2_gnn_bn", "L2_gnn_be", "L3_gnn_b_l0", "L3_gnn_b_l1"]):
                sp.dma_start(BR[:, k, :], a[b].partition_broadcast(P)).then_inc(s_w, 16)
            sp.dma_start(BR[:, 6, :], a["L2_gnn_resid"][0, :].partition_broadcast(P)).then_inc(s_w, 16)
            sp.wait_ge(s_pad, 1)
            for t, name in ((srcI, "src"), (dstI, "dst")):
                v = t[:, :].rearrange("p (g j) -> p g j", j=J)
                sp.dma_start(v[:, 0:NG - 1, :], a[name][0:(NG - 1) * GE].rearrange("(g p j) -> p g j", p=P, j=J)).then_inc(s_idx, 16)
                sp.dma_start(v[0:PTAIL, NG - 1, :], a[name][(NG - 1) * GE:E].rearrange("(p j) -> p j", j=J)).then_inc(s_idx, 16)
            sp.dma_start(blk(XN)[:, 0:NB - 1, :], rows(a["x"][0:(NB - 1) * P, :])).then_inc(s_x, 16)
            sp.dma_start(blk(XN)[0:NTAIL, NB - 1, :], a["x"][(NB - 1) * P:N, :]).then_inc(s_x, 16)

            def tables(p, h, g0):
                sp.dma_start(rows(Hd), h).then_inc(s_tab[p], 16)
                sp.dma_start(rows(Gd), g0).then_inc(s_tab[p], 16)

            flat = [P, NB, P]
            zero = zeros[:, :].unsqueeze(1).to_broadcast(flat)
            sp.wait_ge(s_cst, 1)
            tables("cnt", ones[:, :].unsqueeze(1).to_broadcast(flat), zero)
            sp.wait_ge(s_sc["cnt"], 16 * NT)
            with nc.allow_non_contiguous_dma(reason="one word of each row"):
                sp.dma_start(CN[:, :], rows(Gd)[:, :, 0]).then_inc(s_cn, 16)
            sp.wait_ge(s_cn, 16)
            sp.wait_ge(s_deg, 2)
            with nc.allow_non_contiguous_dma(reason="a word of each node"):
                sp.dma_start(dinv_d.rearrange("(b p) -> p b", p=P), dinv[:, :]).then_inc(s_dv, 16)
                sp.dma_start(rc_d.rearrange("(b p) -> p b", p=P), rc[:, :]).then_inc(s_dv, 16)
            sp.wait_ge(s_dv, 32)
            sp.dma_start(RB[:, :], dinv_d.partition_broadcast(P)).then_inc(s_rb, 16)

            def attr_tile(g, j, t, n):
                sp.wait_ge(s_held, t + 1)
                if n == P:
                    sp.dma_start(at[0:n, 0:DE], a["edge_attr_64"][ds(g * GE, GE), :].rearrange("(p j) f -> p j f", j=J)[:, ds(j, 1), :]).then_inc(s_attr, 16)
                else:
                    sp.dma_start(at[0:n, 0:DE], a["edge_attr_64"][g * GE:E, :].rearrange("(p j) f -> p j f", j=J)[:, ds(j, 1), :]).then_inc(s_attr, 16)

            tables("attr", blk(HN), zero)
            tiles(sp, attr_tile)
            sp.wait_ge(s_sc["attr"], 16 * NT)
            sp.dma_start(Ed[:, :], Gd[:, :]).then_inc(s_dv, 16)
            sp.wait_ge(s_dv, 48)
            sp.wait_ge(s_x, 32)
            for p in range(8):
                if p:
                    sp.wait_ge(s_h, 7 * p)
                h = blk(XN if p in (0, 6) else HN)
                tables(p, h, h if p in SELF else zero)
                sp.wait_ge(s_sc[p], 16 * NT)
                if p == 4:
                    sp.dma_start(blk(AGN), rows(Ed)).then_inc(s_agn, 16)
                    sp.wait_ge(s_ax, agu(4))
                sp.dma_start(blk(AGN), rows(Gd)).then_inc(s_agn, 16)
                sp.wait_ge(s_agn, 16 * (p + 1 + (p >= 4)))
                if p == 5:
                    sp.wait_ge(s_yf, YU[5] + 7)
                    sp.dma_start(RB[:, :], rc_d.partition_broadcast(P)).then_inc(s_rb, 16)
            sp.wait_ge(s_h, 7 * 8)
            sp.dma_start(rows(out[0:(NB - 1) * P, :]), blk(XN)[:, 0:NB - 1, :]).then_inc(s_out, 16)
            sp.dma_start(out[(NB - 1) * P:N, :], blk(XN)[0:NTAIL, NB - 1, :]).then_inc(s_out, 16)
            sp.wait_ge(s_out, 32)

        @block.gpsimd
        def _(pool):
            nc.gpsimd.memset(srcI[:, (NG - 1) * J:], 0)
            nc.gpsimd.memset(XN[:, (NB - 1) * P:], 0.0)
            nc.gpsimd.memset(dstI[:, (NG - 1) * J:], PADNODE).then_inc(s_pad, 1)
            nc.gpsimd.memset(zeros[:, :], 0.0)
            nc.gpsimd.memset(at[:, :], 0.0)
            nc.gpsimd.memset(ones[:, :], 1.0)
            pool.drain()
            nc.gpsimd.affine_select(out=ident[:, :], in_=ones[:, :], compare_op=ALU.is_equal, fill=0.0, base=0,
                                    pattern=[[1, P]], channel_multiplier=-1)
            nc.gpsimd.affine_select(out=low[:, :], in_=ones[:, :], compare_op=ALU.is_gt, fill=0.0, base=0,
                                    pattern=[[-1, P]], channel_multiplier=1).then_inc(s_cst, 1)
            for p in PASSES:
                pool.wait_ge(s_tab[p], 32)

                def tile(g, j, t, n):
                    pool.wait_ge(s_stage[p], t + 1)
                    pool.sem_inc(s_scrap, 1)
                    nc.gpsimd.indirect_dma_start(out=msg[:, :], out_offset=None, in_=Hd[:, :],
                                                 in_offset=bass.IndirectOffsetOnAxis(ap=si[:, 0:1], axis=0)).then_inc(s_g[p], 16)
                    nc.gpsimd.indirect_dma_start(out=old[:, :], out_offset=None, in_=Gd[:, :],
                                                 in_offset=bass.IndirectOffsetOnAxis(ap=di[:, 0:1], axis=0)).then_inc(s_old[p], 16)
                    pool.wait_ge(s_new[p], t + 1)
                    pool.sem_inc(s_scrap, 1)
                    nc.gpsimd.indirect_dma_start(out=Gd[:, :], out_offset=bass.IndirectOffsetOnAxis(ap=xi[:, 0:1], axis=0),
                                                 in_=new[:, :], in_offset=None, bounds_check=NP - 1,
                                                 oob_is_err=False).then_inc(s_sc[p], 16)

                tiles(pool, tile)

        @block.vector
        def _(dve):
            v = nc.vector
            dve.wait_ge(s_idx, 64)
            v.tensor_copy(dstF[:, :], dstI[:, :]).then_inc(s_dst, 1)
            dve.wait_ge(s_cst, 1)
            dve.wait_ge(s_w, 16 * 24)
            dve.wait_ge(s_wt, 1)
            v.tensor_copy(WT[:, :, :].rearrange("p k f -> p (k f)"), X[:, 0:6 * P]).then_inc(s_wc, 1)
            dve.drain()

            def spread(p):
                def tile(g, j, t, n):
                    v.tensor_copy(si[:, :], srcI[:, ds(t, 1)])
                    v.tensor_copy(di[:, :], dstI[:, ds(t, 1)])
                    v.tensor_scalar(Dg[:, :], ident[:, :], dstF[:, ds(t, 1)], None, ALU.mult).then_inc(s_stage[p], 1)
                    dve.wait_ge(s_bc[p], t + 1)
                    v.tensor_scalar(M[:, :], PB, dstF[:, ds(t, 1)], None, ALU.is_equal)
                    dve.drain()
                    v.tensor_tensor_reduce(out=ML[:, :], in0=M[:, :], in1=low[:, :], scale=1.0, scalar=0.0,
                                           op0=ALU.mult, op1=ALU.add, accum_out=cl[:, :])
                    dve.drain()
                    v.tensor_scalar(far[:, :], cl[:, :], 0.5, FAR, ALU.is_gt, ALU.mult)
                    dve.drain()
                    dve.wait_ge(s_g[p], 16 * (t + 1))
                    if p == "attr":
                        v.tensor_tensor(xi[:, :], far[:, :], dstF[:, ds(t, 1)], ALU.add)
                        dve.wait_ge(s_attr, 16 * (t + 1))
                        v.tensor_tensor(msg[:, :], msg[:, :], at[:, :], ALU.mult).then_inc(s_m[p], 1)
                        dve.drain().then_inc(s_held, 1)
                    else:
                        v.tensor_tensor(xi[:, :], far[:, :], dstF[:, ds(t, 1)], ALU.add).then_inc(s_m[p], 1)
                    dve.wait_ge(s_cmb[p], t + 1)
                    dve.sem_inc(s_scrap, 1)
                    dve.wait_ge(s_old[p], 16 * (t + 1))
                    v.tensor_tensor(new[:, :], PC, old[:, :], ALU.add).then_inc(s_new[p], 1)
                    dve.wait_ge(s_sc[p], 16 * (t + 1))
                    dve.sem_inc(s_scrap, 1)

                tiles(dve, tile)

            spread("cnt")
            dve.wait_ge(s_cn, 16)
            v.tensor_scalar(c1[:, :], CN[:, :], 1.0, None, ALU.add).then_inc(s_sq, 1)
            v.tensor_scalar(c2[:, :], CN[:, :], 1.0, None, ALU.max)
            dve.wait_ge(s_sr, 1)
            v.reciprocal(dinv[:, :], SQ[:, :])
            dve.drain()
            v.reciprocal(idg[:, :], c1[:, :])
            v.reciprocal(rc[:, :], c2[:, :]).then_inc(s_deg, 1)
            v.tensor_copy(blk(HN), dinv[:, :].unsqueeze(2).to_broadcast([P, NB, P])).then_inc(s_deg, 1)
            dve.drain().then_inc(s_held, 1)
            dve.drain()
            spread("attr")

            def three(ap):
                return ap.rearrange("p (b f) -> p b f", f=P)

            def row(k):
                return BR[:, k, :].unsqueeze(1).to_broadcast([P, QB, P])

            def of(t, q):
                return t[:, ds(q * QB, QB)].unsqueeze(2).to_broadcast([P, QB, P])

            def norm(p, q):
                for b in range(QB):
                    v.bn_stats(ST[:, b, :], T1[:, b * P:(b + 1) * P])
                dve.drain()
                for b in range(QB):
                    v.bn_aggr(MV[:, b, :], ST[:, b, :])
                dve.drain()
                v.tensor_scalar(VE[:, :], MV[:, :, 1], EPS, None, ALU.add).then_inc(s_var, 1)
                dve.wait_ge(s_sd, LU[p] + q + 1)
                v.reciprocal(RS[:, :], SD[:, :])
                dve.drain()
                for b in range(QB):
                    last = v.tensor_scalar(XN[:, ds(q * QN + b * P, P)], T1[:, b * P:(b + 1) * P], MV[:, b, 0:1], RS[:, b:b + 1],
                                           ALU.subtract, ALU.mult)
                return last

            def y_full(n):
                dve.drain()
                dve.wait_ge(s_yf, n)

            for p in range(8):
                spread(p)
                if p in (1, 2, 3, 6, 7):
                    dve.wait_ge(s_rb, 16 if p < 4 else 32)
                with dve.Fori(0, NQ) as q:
                    dve.wait_ge(s_ax, agu(p) + q + 1)
                    cols = ds(q * QN, QN)
                    if p in (1, 2, 3, 6, 7):
                        v.tensor_tensor(AT[:, cols], X[:, 0:QN], RB[:, cols], ALU.mult).then_inc(s_at, 1)
                    else:
                        v.tensor_copy(AT[:, cols], X[:, 0:QN]).then_inc(s_at, 1)
                    dve.drain().then_inc(s_axf, 1)
                with dve.Fori(0, NQ) as q:
                    cols = ds(q * QN, QN)
                    y_full(YU[p] + q + 1)
                    y = three(Y[:, 0:QN])
                    t1 = three(T1[:, :])
                    if p == 0:
                        v.tensor_tensor(t1, y, row(0), ALU.add).then_inc(s_yfree, 1)
                        dve.drain()
                        v.scalar_tensor_tensor(out=T1[:, :], in0=T1[:, :], scalar=0.0, in1=XN[:, cols], op0=ALU.max, op1=ALU.add)
                        dve.drain()
                        norm(p, q)
                        dve.drain()
                        v.tensor_tensor(three(HN[:, cols]), three(XN[:, cols]), of(dinv, q), ALU.mult).then_inc(s_h, 1)
                    elif p in (1, 2, 3):
                        v.tensor_tensor(three(HN[:, cols]), y, of(dinv, q), ALU.mult).then_inc(s_h, 1)
                        dve.drain().then_inc(s_yfree, 1)
                    elif p == 4:
                        v.tensor_tensor(t1, y, of(dinv, q), ALU.mult).then_inc(s_yfree, 1)
                        dve.drain()
                        v.tensor_tensor(t1, t1, row(1), ALU.add)
                        dve.drain()
                        v.tensor_tensor(T1[:, :], T1[:, :], XN[:, cols], ALU.add)
                        dve.drain()
                        norm(p, q).then_inc(s_xn, 1)
                    elif p == 5:
                        v.tensor_tensor(t1, y, of(dinv, q), ALU.mult).then_inc(s_yfree, 1)
                        dve.drain()
                        v.tensor_tensor(T1[:, :], T1[:, :], XN[:, cols], ALU.add)
                        dve.drain()
                        v.tensor_tensor(T1[:, :], T1[:, :], HR[:, cols], ALU.add)
                        dve.drain()
                        norm(p, q).then_inc(s_xn, 1)
                        dve.drain().then_inc(s_h, 1)
                    elif p == 6:
                        v.tensor_tensor(t1, y, row(4), ALU.add).then_inc(s_yfree, 1)
                        dve.drain()
                        v.tensor_scalar(HN[:, cols], T1[:, :], 0.0, None, ALU.max).then_inc(s_h, 1)
                    else:
                        v.tensor_tensor(t1, y, row(5), ALU.add).then_inc(s_yfree, 1)
                        dve.drain()
                        v.tensor_tensor(T1[:, :], T1[:, :], XN[:, cols], ALU.add)
                        dve.drain()
                        norm(p, q).then_inc(s_h, 1)
                if p == 4:
                    with dve.Fori(0, NQ) as q:
                        cols = ds(q * QN, QN)
                        y_full(YU[4] + 7 + q + 1)
                        v.tensor_tensor(three(T1[:, :]), three(Y[:, 0:QN]), row(2), ALU.add).then_inc(s_yfree, 1)
                        dve.drain()
                        v.tensor_tensor(three(HN[:, cols]), three(T1[:, :]), row(3), ALU.add)
                        v.tensor_tensor(three(HR[:, cols]), three(T1[:, :]), row(6), ALU.add)
                        dve.drain()
                        v.tensor_tensor(three(HR[:, cols]), three(HR[:, cols]), of(idg, q), ALU.mult)
                        v.tensor_tensor(three(HN[:, cols]), three(HN[:, cols]), of(dinv, q), ALU.mult).then_inc(s_h, 1)

        @block.scalar
        def _(act):
            s = nc.scalar
            act.wait_ge(s_sq, 1)
            s.activation(SQ[:, :], c1[:, :], ACT.Sqrt).then_inc(s_sr, 1)

            def root(n):
                act.wait_ge(s_var, n)
                s.activation(SD[:, :], VE[:, :], ACT.Sqrt).then_inc(s_sd, 1)

            for p in range(8):
                if p == 4:
                    with act.Fori(0, NQ) as q:
                        act.wait_ge(s_ax, agu(4) - 7 + q + 1)
                        s.copy(RB[:, ds(q * QN, QN)], X[:, 0:QN]).then_inc(s_ea, 1)
                        act.drain().then_inc(s_axf, 1)
                if p in (0, 1):
                    with act.Fori(0, NQ) as q:
                        act.wait_ge(s_xf, XU[p] + q + 1)
                        for h in range(2):
                            last = s.activation(TB[:, ds(q * QN + h * UN, UN)], X[:, 512 * h:512 * h + UN], ACT.Relu,
                                                bias=BC[:, p:p + 1])
                        last.then_inc(s_tb, 1)
                        act.drain().then_inc(s_xfree, 1)
                        if p == 0:
                            root(LU[p] + q + 1)
                elif p in (2, 3):
                    with act.Fori(0, NQ) as q:
                        act.wait_ge(s_at, 7 * p + q + 1)
                        cols = ds(q * QN, QN)
                        s.activation(TB[:, cols], AT[:, cols], ACT.Relu, bias=BC[:, p:p + 1]).then_inc(s_tb, 1)
                elif p in (4, 5, 6):
                    with act.Fori(0, NQ) as q:
                        if p < 6:
                            root(LU[p] + q + 1)
                        act.wait_ge(s_zf, ZU[p] + q + 1)
                        s.copy(TB[:, ds(q * QN, QN)], Z[:, 0:QN]).then_inc(s_tb, 1)
                        act.drain().then_inc(s_zfree, 1)
                else:
                    with act.Fori(0, NQ) as q:
                        root(LU[p] + q + 1)

        @block.tensor
        def _(pe):
            t_ = nc.tensor
            pe.wait_ge(s_cst, 1)
            pe.wait_ge(s_w, 16 * 24)
            for k in range(6):
                last = t_.transpose(X[:, k * P:(k + 1) * P], WR[:, k, :], ident[:, :])
            last.then_inc(s_wt, 1)
            pe.wait_ge(s_wc, 1)
            pe.sem_inc(s_xfree, 1)
            pe.sem_inc(s_yfree, 1)
            pe.sem_inc(s_zfree, 1)
            pe.sem_inc(s_axf, 1)

            def spread(p):
                def tile(g, j, t, n):
                    pe.wait_ge(s_stage[p], t + 1)
                    t_.matmul(PB, ones[:, :], Dg[:, :], start=True, stop=True).then_inc(s_bc[p], 1)
                    pe.wait_ge(s_m[p], t + 1)
                    t_.matmul(PC, M[:, :], msg[:, :], start=True, stop=True).then_inc(s_cmb[p], 1)

                tiles(pe, tile)

            def sums(n, loaded):
                pe.wait_ge(s_agn, 16 * loaded)
                for q in range(NQ):
                    pe.wait_ge(s_axf, n + q + 1)
                    for b in range(QB):
                        last = t_.transpose(X[:, b * P:(b + 1) * P], AGN[:, ds(q * QN + b * P, P)], ident[:, :])
                    last.then_inc(s_ax, 1)

            def node_stage(n, q, parts):
                pe.wait_ge(s_yfree, n + q + 1)
                for b in range(QB):
                    for k, (t, w, rows_) in enumerate(parts):
                        last = t_.matmul(Y[:, b * P:(b + 1) * P], t[0:rows_, ds(q * QN + b * P, P)], w,
                                         start=k == 0, stop=k == len(parts) - 1)
                last.then_inc(s_yf, 1)

            def turn(p, q, source):
                pe.wait_ge(s_zfree, ZU[p] + q + 1)
                for b in range(QB):
                    last = t_.transpose(Z[:, b * P:(b + 1) * P], source[:, ds(q * QN + b * P, P)], ident[:, :])
                last.then_inc(s_zf, 1)

            for p in PASSES:
                spread(p)
                if p in ("cnt", "attr"):
                    continue
                if p == 4:
                    sums(agu(4) - 7, 5)
                sums(agu(p), p + 1 + (p >= 4))
                pe.wait_ge(s_at, 7 * (p + 1))
                if p in (0, 1):
                    w = WT[:, 0, :] if p == 0 else WN[:, 0, :]
                    for q in range(NQ):
                        pe.wait_ge(s_xfree, XU[p] + q + 1)
                        for h in range(2):
                            last = t_.matmul(X[:, 512 * h:512 * h + UN], w, AT[:, ds(q * QN + h * UN, UN)], start=True, stop=True)
                        last.then_inc(s_xf, 1)
                        pe.wait_ge(s_tb, TU[p] + q + 1)
                        node_stage(YU[p], q, [(TB, WT[:, 1, :] if p == 0 else WN[:, 1, :], P)])
                elif p in (2, 3):
                    for q in range(NQ):
                        pe.wait_ge(s_tb, TU[p] + q + 1)
                        node_stage(YU[p], q, [(TB, WN[:, p, :], P)])
                elif p == 4:
                    for q in range(NQ):
                        node_stage(YU[p], q, [(AT, ident[:, :], P)])
                        pe.wait_ge(s_xn, q + 1)
                        turn(p, q, XN)
                    for q in range(NQ):
                        pe.wait_ge(s_tb, TU[p] + q + 1)
                        node_stage(YU[p] + 7, q, [(TB, WN[:, 4, :], P)])
                elif p == 5:
                    pe.wait_ge(s_ea, 7)
                    for q in range(NQ):
                        node_stage(YU[p], q, [(AT, ident[:, :], P), (RB, We2[:, :], P)])
                        pe.wait_ge(s_xn, 7 + q + 1)
                        turn(p, q, XN)
                elif p == 6:
                    pe.wait_ge(s_tb, TU[6])
                    for q in range(NQ):
                        node_stage(YU[p], q, [(AT, WT[:, 2, :], P), (TB, WT[:, 3, :], P)])
                        pe.wait_ge(s_h, 7 * 6 + q + 1)
                        turn(p, q, HN)
                else:
                    pe.wait_ge(s_tb, TU[6] + 7)
                    for q in range(NQ):
                        node_stage(YU[p], q, [(AT, WT[:, 4, :], P), (TB, WT[:, 5, :], P)])


_INS = ['x', 'src', 'dst', 'edge_attr_64', 'L0_gnn_W1', 'L0_gnn_b1', 'L0_gnn_W2', 'L0_gnn_b2', 'L1_gnn_W1', 'L1_gnn_b1',
        'L1_gnn_W2', 'L1_gnn_b2', 'L1_gnn_W3', 'L1_gnn_b3', 'L1_gnn_W4', 'L1_gnn_b4', 'L2_gnn_Wn', 'L2_gnn_bn',
        'L2_gnn_We', 'L2_gnn_be', 'L2_gnn_resid', 'L3_gnn_W_l0', 'L3_gnn_b_l0', 'L3_gnn_W_r0', 'L3_gnn_W_l1',
        'L3_gnn_b_l1', 'L3_gnn_W_r1']


def kernel(**inputs):
    import numpy as _np
    import concourse.bacc as _bacc
    from concourse import mybir as _mybir
    from concourse.bass_utils import run_bass_kernel_spmd as _run

    nc = _bacc.Bacc("TRN2", target_bir_lowering=False, num_devices=1)
    arrays, aps = {}, {}
    for name in _INS:
        v = _np.ascontiguousarray(inputs[name])
        arrays[f"in_{name}_dram"] = v
        aps[name] = nc.dram_tensor(f"in_{name}_dram", v.shape, _mybir.dt.from_np(v.dtype), kind="ExternalInput").ap()
    out = nc.dram_tensor("out_0_dram", inputs["x"].shape, _mybir.dt.float32, kind="ExternalOutput").ap()
    build(nc, aps, out)
    r = _run(nc, [arrays], core_ids=[0])
    return r.results[0]["out_0_dram"]
```

```python
import concourse.bass as bass
from concourse import mybir
from contextlib import ExitStack

P = 128


def build(nc, a, out):
    fp32 = mybir.dt.float32
    i32 = mybir.dt.int32
    f16 = mybir.dt.float16
    ALU = mybir.AluOpType
    ACT = mybir.ActivationFunctionType
    AX = mybir.AxisListType.X
    ds = bass.ds

    N, D = a["x"].shape
    E, DE = a["edge_attr_64"].shape
    NB = -(-N // P)
    NP = NB * P
    NTAIL = N - (NB - 1) * P
    J = 17
    GE = P * J
    NG = -(-E // GE)
    PTAIL = (E - (NG - 1) * GE) // J
    assert PTAIL * J == E - (NG - 1) * GE
    NT = NG * J
    PADNODE = NP - 1
    QB = 7
    NQ = NB // QB
    QN = QB * P
    UN = QN // 2
    EPS = 1e-5
    FAR = 1.0e6

    NU = NP // UN
    UH = NU // 2
    SLOTS = 3 * P
    WIN = 256
    MARGIN = 64
    LAG = 2
    G0 = [next(g for g in range(NG + 1) if g == NG or (P * g - MARGIN) // UN >= s) for s in range(NU + 1)]
    G0[0] = 0
    DLO = [UN * u // P for u in range(NU)]
    CENTRE = 14
    RING = 4
    SR = 4

    Hd = nc.dram_tensor("h_rows", (NP, D), fp32).ap()
    Gd = nc.dram_tensor("sum_rows", (NP, D), fp32).ap()
    Ed = nc.dram_tensor("attr_rows", (NP, D), fp32).ap()
    dinv_d = nc.dram_tensor("dinv_vec", (NP,), fp32).ap()
    rc_d = nc.dram_tensor("rc_vec", (NP,), fp32).ap()
    cnt_d = nc.dram_tensor("cnt_vec", (NP,), fp32).ap()
    Td = nc.dram_tensor("edge_table", (NU * NB * SLOTS, 2), f16).ap()
    Ad = nc.dram_tensor("adjacency", (2, NB, P, UH * UN), f16).ap()

    PASSES = ["cnt", "attr"] + list(range(8))
    SELF = [0, 1, 2, 3, 4]

    with ExitStack() as ctx:
        def sb(name, shape, dt=fp32):
            return ctx.enter_context(nc.sbuf_tensor(name, shape, dt))

        def sem(name):
            return ctx.enter_context(nc.semaphore(name))

        XN = sb("XN", [P, NP])
        HN = sb("HN", [P, NP])
        HR = sb("HR", [P, NP])
        AGN = sb("AGN", [P, NP])
        AT = sb("AT", [P, NP])
        TB = sb("TB", [P, NP])
        RBW = sb("RBW", [P, NP + 2 * MARGIN])
        RB = RBW[:, MARGIN:MARGIN + NP]
        S5 = sb("S5", [P, UH * UN // 2])
        T1 = sb("T1", [P, QN])
        ST = sb("ST", [P, QB, 6])
        MV = sb("MV", [P, QB, 2])
        VE = sb("VE", [P, QB])
        SD = sb("SD", [P, QB])
        RS = sb("RS", [P, QB])
        srcI = sb("srcI", [P, NT], i32)
        dstI = sb("dstI", [P, NT], i32)
        dstF = sb("dstF", [P, NT])
        ident = sb("ident", [P, P])
        ones = sb("ones", [P, P])
        zeros = sb("zeros", [P, P])
        WR = AT[:, 0:6 * P].rearrange("p (k f) -> p k f", k=6)
        WT = sb("WT", [P, 6, P])
        WN = sb("WN", [P, 5, P])
        We2 = sb("We2", [P, P])
        BC = sb("BC", [P, 4])
        BR = sb("BR", [P, 7, P])
        CN = sb("CN", [P, NB])
        dinv = sb("dinv", [P, NB])
        rc = sb("rc", [P, NB])
        idg = sb("idg", [P, NB])
        c1 = sb("c1", [P, NB])
        c2 = sb("c2", [P, NB])
        SQ = sb("SQ", [P, NB])
        si = sb("si", [P, 1], i32)
        di = sb("di", [P, 1], i32)
        xi = sb("xi", [P, 1], i32)
        Dg, M, ML, msg, old, new, at, low = (S5[:, k * P:(k + 1) * P] for k in range(8))
        cl = sb("cl", [P, 1])
        far = sb("far", [P, 1])
        HI = AGN[:, 0:NP // 2].bitcast(f16)
        LO = AGN[:, NP // 2:NP].bitcast(f16)
        MX = sb("MX", [P, NQ])
        mx = sb("mx", [P, 1])
        m1 = sb("m1", [1, 1])
        mc = sb("mc", [P, 1])
        me = sb("me", [P, 1], i32)
        SC = sb("SC", [P, 9, 2])
        iot = sb("iot", [P, UN], f16)
        iok = sb("iok", [P, 2, NB], f16)
        Lt = sb("Lt", [P, P], f16)
        Uc = sb("Uc", [P, P], f16)
        I16 = sb("I16", [P, P], f16)
        O16 = sb("O16", [P, P], f16)
        valid = sb("valid", [P, J])
        fl = sb("fl", [P, 4])
        flag = sb("flag", [P, 1], i32)
        gwin = sb("gwin", [P, NG])
        MXE = T1[:, 0:NG]
        NS = dstI[:, :].bitcast(fp32)
        sni = sb("sni", [P, 2, J], i32)
        nsv = sb("nsv", [P, 2, J])
        KEY, BASE, RK, CAP, PAYW, UU, SB = (HR[:, k * NT:(k + 1) * NT] for k in range(7))
        PAY = PAYW.bitcast(f16).rearrange("p (t c) -> p t c", c=2)
        off = [0]

        def carve(cols, shape=None, dt=f16):
            w = cols // (2 if dt == f16 else 1)
            v = TB[:, off[0]:off[0] + w]
            off[0] += w
            return v.bitcast(f16) if dt == f16 else (v.bitcast(dt) if dt != fp32 else v)

        OHK = [[carve(2 * NB) for _ in range(4)] for _ in range(2)]
        OHS = [[carve(P) for _ in range(3)] for _ in range(3)]
        OHD = [[carve(UN) for _ in range(3)] for _ in range(3)]
        A16 = [[carve(UN) for _ in range(3)] for _ in range(2)]
        TAB = [carve(2 * SLOTS) for _ in range(2)]
        SLD = [carve(6 * NB, dt=fp32).rearrange("p (k n) -> p k n", n=NB) for _ in range(2)]
        JK = [carve(2 * NB) for _ in range(4)]
        POS = [carve(4, dt=i32) for _ in range(SR)]
        PST = [carve(8).rearrange("p (a c) -> p a c", c=2) for _ in range(SR)]
        TI = HN[:, 0:NT].bitcast(i32)
        TF = HN[:, NT:2 * NT]
        TG = HN[:, 2 * NT:3 * NT]
        FILL = HN[:, 3 * NT:3 * NT + NU * NB * SLOTS // P].bitcast(f16)
        AE = [TB[:, k * J * DE:(k + 1) * J * DE] for k in range(2)]
        AHL = [HN[:, k * J * DE:(k + 1) * J * DE].bitcast(f16).rearrange("p (j f) -> p j f", j=J) for k in range(2)]
        OHW = [HN[:, (k + 1) * J * P:(k + 2) * J * P].bitcast(f16).rearrange("p (j f) -> p j f", j=J) for k in range(1)]
        OHW.append(TB[:, J * P:2 * J * P].bitcast(f16).rearrange("p (j f) -> p j f", j=J))

        PS = ctx.enter_context(nc.psum_tensor("PS", [P, 4096], fp32))
        RP = PS[:, 0:1024]
        BP = [PS[:, 512 * (2 + k):512 * (2 + k) + UN] for k in range(3)]
        AGG, CNT = PS[:, 2560:2560 + UN], PS[:, 3072:3072 + UN]
        TP = PS[:, 3584:4096].bitcast(f16)
        CH = PS[:, 3584:4096]
        WTP = PS[:, 2560:2560 + 6 * P]
        AGB = [PS[:, 512 * k:512 * k + UN] for k in range(UH)]
        X, Y, Z = PS[:, 0:1024], PS[:, 1024:2048], PS[:, 2048:3072]
        PB, PC = PS[:, 3072:3072 + P], PS[:, 3584:3584 + P]

        s_w = sem("weights_loaded")
        s_cst = sem("constants_ready")
        s_idx = sem("indices_loaded")
        s_pad = sem("pads_set")
        s_dst = sem("dst_float")
        s_wt = sem("weights_transposed")
        s_wc = sem("weights_copied")
        s_x = sem("x_loaded")
        s_tab = {p: sem(f"tables_{p}") for p in PASSES}
        s_g = {p: sem(f"gathered_{p}") for p in PASSES}
        s_old = {p: sem(f"old_{p}") for p in PASSES}
        s_stage, s_bc, s_m, s_cmb, s_new = (sem(n) for n in ("staged", "dst_row", "match", "combined", "new"))
        s_sc = {p: sem(f"scattered_{p}") for p in PASSES}
        s_attr = sem("attr_tile")
        s_held = sem("held")
        s_scrap = sem("scrap")
        s_cn = sem("cnt_loaded")
        s_sq = sem("cnt_plus_one")
        s_sr = sem("cnt_root")
        s_deg = sem("degree_factors")
        s_dv = sem("factors_stored")
        s_rb = sem("factor_row_loaded")
        s_agn = sem("sums_loaded")
        s_ax = sem("sums_transposed")
        s_axf = sem("sums_transposed_free")
        s_at = sem("AT_ready")
        s_ea = sem("EA_ready")
        s_xf, s_xfree = sem("X_full"), sem("X_free")
        s_yf, s_yfree = sem("Y_full"), sem("Y_free")
        s_zf, s_zfree = sem("Z_full"), sem("Z_free")
        s_tb = sem("TB_ready")
        s_var = sem("variance")
        s_sd = sem("deviation")
        s_xn = sem("XN_ready")
        s_h = sem("H_ready")
        s_out = sem("stored")
        s_key = sem("keys_ready")
        s_fill = sem("fill_ready")
        s_init = sem("table_cleared")
        s_oh, s_rp, s_rk = sem("key_hot"), sem("rank_counts"), sem("rank_read")
        s_pos, s_pay = sem("positions_staged"), sem("payload_staged")
        s_sct = [sem(f"edges_scattered_{r}") for r in range(SR)]
        s_tabl = [sem("table_loaded_0"), sem("table_loaded_1")]
        s_tt, s_sld = sem("table_turned"), sem("bucket_edges_ready")
        s_ohb, s_bm, s_ev8, s_spm = sem("edge_hot"), sem("block_counted"), sem("block_copied"), sem("block_used")
        s_aw = [[sem(f"block_stored_{b}{a_}") for a_ in range(3)] for b in range(2)]
        s_un = sem("unit_summed")
        s_f1, s_f2, s_flag = sem("flag_parts"), sem("flag_summed"), sem("flag_ready")
        s_at0 = sem("AT_ready_general")
        s_c1, s_c2, s_c3, s_c4 = sem("max_lane"), sem("max_row"), sem("max_one"), sem("max_spread")
        s_hi, s_split = sem("high_ready"), sem("split_ready")
        s_al = [sem(f"adjacency_loaded_{k}") for k in range(RING + 1)]
        s_af = [sem(f"adjacency_free_{k}") for k in range(RING + 1)]
        s_agg = sem("half_summed")
        s_ael = [sem("edge_features_loaded_0"), sem("edge_features_loaded_1")]
        s_aem = sem("edge_features_measured")
        s_nst, s_nsg, s_nsc = sem("source_index_staged"), [sem("source_factor_0"), sem("source_factor_1")], sem("source_factor_copied")
        s_ahl, s_eam, s_eae = sem("edge_split"), sem("edges_summed"), sem("edge_sums_added")
        s_cv = sem("cnt_stored")
        s_d1, s_d2, s_d3, s_d4 = sem("edge_max_lane"), sem("edge_max_row"), sem("edge_max_one"), sem("edge_max_spread")
        s_scale = sem("scale_ready")
        s_aes, s_ahi = sem("edge_features_scaled"), sem("edge_high_ready")

        XU = {0: 0, 1: 7}
        YU = {0: 0, 1: 7, 2: 14, 3: 21, 4: 28, 5: 42, 6: 49, 7: 56}
        ZU = {4: 0, 5: 7, 6: 14}
        TU = {0: 0, 1: 7, 2: 14, 3: 21, 4: 28, 5: 35, 6: 42}
        LU = {0: 0, 4: 7, 5: 14, 7: 21}
        MEASURED = [0, 2, 3, 4, 5, 7]
        SMALL = [1, 6]
        EDGES = 8
        CU = {p: (k, (s_c1, s_c2, s_c3, s_c4)) for k, p in enumerate([0, 2, 3, 4, 5, 7])}
        CU[EDGES] = (0, (s_d1, s_d2, s_d3, s_d4))

        def agu(p):
            return 7 * p + (7 if p >= 4 else 0)

        def atu(p):
            return NU * p

        NGS = [G0[s + 1] - G0[s] for s in range(NU)]

        def scattered(s, r, it=None):
            n = 16 * sum(len(range(r, J, SR)) * NGS[x] for x in range(min(s, NU)))
            return n if it is None else n + (it - r) * (16 // SR) * NGS[s]

        def ahead(u):
            out_ = []
            for b in range(DLO[u], min(DLO[u] + 4, NB)):
                lo, hi = max(P * b, UN * u), min(P * b + P, UN * u + UN)
                if lo < hi:
                    out_.append((b, lo - P * b, lo - UN * u, hi - lo))
            return out_

        def ring(p):
            r = (TB if p == 5 else HR)[:, :].bitcast(f16)
            return [r[:, k * UH * UN:(k + 1) * UH * UN] for k in range(RING)] + [S5[:, :].bitcast(f16)]

        def iterations(eng, body):
            for r in range(SR):
                body(r, r)
            with eng.Fori(1, J // SR) as i:
                for r in range(SR):
                    body(SR * i + r, r)
            body(J - 1, 0)

        def builds(it):
            return 1 if isinstance(it, int) and it == 16 else 3

        def slots_of(it, a_):
            return 3 if isinstance(it, int) and 3 * it + a_ < 4 else 2

        def half_of(it):
            return it // 2 if isinstance(it, int) else None

        block = ctx.enter_context(nc.Block())

        def tiles(eng, body):
            with eng.Fori(0, NG - 1) as g:
                with eng.Fori(0, J) as j:
                    body(g, j, g * J + j, P)
            with eng.Fori(0, J) as j:
                body(NG - 1, j, (NG - 1) * J + j, PTAIL)

        def rows(t):
            return t.rearrange("(b p) f -> p b f", p=P)

        def blk(t):
            return t[:, :].rearrange("p (b f) -> p b f", f=P)

        flags = {}

        def read_flag(eng, name):
            eng.wait_ge(s_flag, 1)
            flags[name] = eng.value_load(flag[0:1, 0:1], min_val=0, max_val=1)

        @block.sync
        def _(sp):
            sp.wait_ge(s_pad, 1)
            for t, name in ((srcI, "src"), (dstI, "dst")):
                v = t[:, :].rearrange("p (g j) -> p g j", j=J)
                sp.dma_start(v[:, 0:NG - 1, :], a[name][0:(NG - 1) * GE].rearrange("(g p j) -> p g j", p=P, j=J)).then_inc(s_idx, 16)
                sp.dma_start(v[0:PTAIL, NG - 1, :], a[name][(NG - 1) * GE:E].rearrange("(p j) -> p j", j=J)).then_inc(s_idx, 16)
            sp.wait_ge(s_fill, 1)
            sp.dma_start(Td.rearrange("(p r) c -> p (r c)", p=P), FILL).then_inc(s_init, 16)
            sp.dma_start(blk(XN)[:, 0:NB - 1, :], rows(a["x"][0:(NB - 1) * P, :])).then_inc(s_x, 16)
            sp.dma_start(blk(XN)[0:NTAIL, NB - 1, :], a["x"][(NB - 1) * P:N, :]).then_inc(s_x, 16)
            for k, w in enumerate(["L0_gnn_W1", "L0_gnn_W2", "L3_gnn_W_l0", "L3_gnn_W_r0", "L3_gnn_W_l1", "L3_gnn_W_r1"]):
                sp.dma_start(WR[:, k, :], a[w][:, :]).then_inc(s_w, 16)
            for k, w in enumerate(["L1_gnn_W1", "L1_gnn_W2", "L1_gnn_W3", "L1_gnn_W4", "L2_gnn_Wn"]):
                sp.dma_start(WN[:, k, :], a[w][:, :]).then_inc(s_w, 16)
            for k in range(2):
                sp.dma_start(We2[DE * k:DE * k + DE, :], a["L2_gnn_We"][:, :]).then_inc(s_w, 16)
            with nc.allow_non_contiguous_dma(reason="a bias of 128 words on partitions"):
                for k, b in enumerate(["L0_gnn_b1", "L1_gnn_b1", "L1_gnn_b2", "L1_gnn_b3"]):
                    sp.dma_start(BC[:, k:k + 1], a[b].rearrange("(p o) -> p o", o=1)).then_inc(s_w, 16)
            for k, b in enumerate(["L0_gnn_b2", "L1_gnn_b4", "L2_gnn_bn", "L2_gnn_be", "L3_gnn_b_l0", "L3_gnn_b_l1"]):
                sp.dma_start(BR[:, k, :], a[b].partition_broadcast(P)).then_inc(s_w, 16)
            sp.dma_start(BR[:, 6, :], a["L2_gnn_resid"][0, :].partition_broadcast(P)).then_inc(s_w, 16)

            for s in range(NU + LAG):
                if 1 <= s <= NU:
                    u = s - 1
                    for r in range(SR):
                        sp.wait_ge(s_sct[r], scattered(s, r))
                    if u >= 2:
                        sp.wait_ge(s_tt, u - 1)
                    t = Td.rearrange("(u n r) c -> u n (r c)", u=NU, n=NB)[u]
                    for n0, sb0, n in ((0, DLO[u], NB - DLO[u]), (NB - DLO[u], 0, DLO[u])):
                        if n:
                            sp.dma_start(TAB[u % 2][n0:n0 + n, :], t[sb0:sb0 + n, :]).then_inc(s_tabl[u % 2], 16)
                u = s - LAG
                if u < 0:
                    continue

                def store(it, r):
                    b = r % 2
                    for a_ in range(builds(it)):
                        n = 3 * it + a_
                        sp.wait_ge(s_ev8, NB * u + n + 1)
                        k = (n + DLO[u]) % NB
                        sp.dma_start(Ad[u // UH][ds(k, 1) if not isinstance(k, int) else slice(k, k + 1), :,
                                                 (u % UH) * UN:(u % UH + 1) * UN].rearrange("o p c -> p (o c)"),
                                     A16[b][a_]).then_inc(s_aw[b][a_], 16)

                iterations(sp, store)
            for b in range(2):
                for a_ in range(3):
                    sp.wait_ge(s_aw[b][a_], 16 * NU * (9 if (b, a_) == (0, 0) else 8))
            read_flag(sp, "sp")

            def tables(p, h, g0):
                sp.dma_start(rows(Hd), h).then_inc(s_tab[p], 16)
                sp.dma_start(rows(Gd), g0).then_inc(s_tab[p], 16)

            flat = [P, NB, P]
            zero = zeros[:, :].unsqueeze(1).to_broadcast(flat)

            def attr_tile(g, j, t, n):
                sp.wait_ge(s_held, t + 1)
                size = GE if n == P else E - (NG - 1) * GE
                sp.dma_start(at[0:n, 0:DE], a["edge_attr_64"][ds(g * GE, size) if n == P else slice(g * GE, E), :]
                             .rearrange("(p j) f -> p j f", j=J)[:, ds(j, 1), :]).then_inc(s_attr, 16)

            def general(p):
                h = blk(XN if p in (0, 6) else HN)
                tables(p, h, h if p in SELF else zero)
                sp.wait_ge(s_sc[p], 16 * NT)
                sp.wait_ge(s_split, 7 * p + 7)
                if p == 4:
                    sp.dma_start(blk(AGN), rows(Ed)).then_inc(s_agn, 16)
                    sp.wait_ge(s_ax, agu(4))
                sp.dma_start(blk(AGN), rows(Gd)).then_inc(s_agn, 16)
                sp.wait_ge(s_agn, 16 * (p + 1 + (p >= 4)))

            with sp.If(flags["sp"]):
                tables("cnt", ones[:, :].unsqueeze(1).to_broadcast(flat), zero)
                sp.wait_ge(s_sc["cnt"], 16 * NT)
                with nc.allow_non_contiguous_dma(reason="one word of each row"):
                    sp.dma_start(CN[:, :], rows(Gd)[:, :, 0]).then_inc(s_cn, 16)
                    sp.wait_ge(s_cn, 16)
                    sp.dma_start(cnt_d.rearrange("(b p) -> p b", p=P), CN[:, :]).then_inc(s_cv, 16)
            with sp.Else():
                sp.wait_ge(s_at, NU)
                sp.dma_start(cnt_d.rearrange("(o n) -> o n", o=1), RB[0:1, :]).then_inc(s_cv, 16)
                sp.sem_inc(s_cn, 16)
            sp.wait_ge(s_cv, 16)
            with nc.allow_non_contiguous_dma(reason="a word of each node"):
                sp.dma_start(CN[:, :], cnt_d.rearrange("(b p) -> p b", p=P)).then_inc(s_cn, 16)
                sp.wait_ge(s_deg, 2)
                sp.dma_start(dinv_d.rearrange("(b p) -> p b", p=P), dinv[:, :]).then_inc(s_dv, 16)
                sp.dma_start(rc_d.rearrange("(b p) -> p b", p=P), rc[:, :]).then_inc(s_dv, 16)
            sp.wait_ge(s_dv, 32)
            sp.dma_start(RB, dinv_d.partition_broadcast(P)).then_inc(s_rb, 16)
            with sp.If(flags["sp"]):
                tables("attr", blk(HN), zero)
                tiles(sp, attr_tile)
                sp.wait_ge(s_sc["attr"], 16 * NT)
                sp.dma_start(Ed[:, :], Gd[:, :]).then_inc(s_dv, 16)
                sp.wait_ge(s_dv, 48)
                general(0)

            def blocks(p):
                slot = ring(p)
                for h in range(2):
                    n = 2 * (p - 1) + h
                    sp.wait_ge(s_af[RING], n + 1)
                    sp.dma_start(slot[RING], Ad[h][0]).then_inc(s_al[RING], 16)
                    with sp.Fori(0, (NB - 1) // RING) as i:
                        for m in range(RING):
                            sp.wait_ge(s_af[m], 12 * n + i + 1)
                            sp.dma_start(slot[m], Ad[h][ds(RING * i + 1 + m, 1), :, :].rearrange("o p c -> p (o c)")).then_inc(s_al[m], 16)

            for p in range(1, 8):
                if p in (5, 6):
                    sp.wait_ge(s_h, 7 * p)
                if p == 6:
                    sp.dma_start(RB, rc_d.partition_broadcast(P)).then_inc(s_rb, 16)
                with sp.If(flags["sp"]):
                    sp.wait_ge(s_h, 7 * p)
                    general(p)
                with sp.Else():
                    blocks(p)
            sp.wait_ge(s_h, 7 * 8)
            sp.dma_start(rows(out[0:(NB - 1) * P, :]), blk(XN)[:, 0:NB - 1, :]).then_inc(s_out, 16)
            sp.dma_start(out[(NB - 1) * P:N, :], blk(XN)[0:NTAIL, NB - 1, :]).then_inc(s_out, 16)
            sp.wait_ge(s_out, 32)

        @block.gpsimd
        def _(pool):
            g_ = nc.gpsimd
            g_.memset(srcI[:, (NG - 1) * J:], 0)
            g_.memset(dstI[:, (NG - 1) * J:], PADNODE).then_inc(s_pad, 1)
            g_.memset(XN[:, (NB - 1) * P:], 0.0)
            g_.memset(FILL, -1.0).then_inc(s_fill, 1)
            g_.memset(valid[:, :], 0.0)
            g_.memset(at, 0.0)
            g_.memset(zeros[:, :], 0.0)
            g_.memset(ones[:, :], 1.0)
            g_.memset(O16[:, :], 1.0)
            for p in SMALL:
                g_.memset(SC[:, p, 0:1], 2.0 ** (CENTRE - 2))
                g_.memset(SC[:, p, 1:2], 2.0 ** (2 - CENTRE))
            for s in range(NU):
                g_.memset(TG[:, G0[s] * J:G0[s + 1] * J], float(s))
            pool.drain()
            g_.memset(valid[0:PTAIL, :], 1.0)
            g_.iota(gwin[:, :], [[P, NG]], base=-MARGIN, channel_multiplier=0, allow_small_or_imprecise_dtypes=True)
            g_.iota(iot[:, :], [[1, UN]], base=0, channel_multiplier=0, allow_small_or_imprecise_dtypes=True)
            g_.iota(iok[:, :, :], [[64, 2], [1, NB]], base=0, channel_multiplier=0, allow_small_or_imprecise_dtypes=True)
            g_.affine_select(out=Lt[:, :], in_=O16[:, :], compare_op=ALU.is_gt, fill=0.0, base=0, pattern=[[1, P]], channel_multiplier=-1)
            g_.affine_select(out=Uc[:, :], in_=O16[:, :], compare_op=ALU.is_ge, fill=0.0, base=0, pattern=[[-1, P]], channel_multiplier=1)
            g_.affine_select(out=I16[:, :], in_=O16[:, :], compare_op=ALU.is_equal, fill=0.0, base=0, pattern=[[1, P]], channel_multiplier=-1)
            g_.affine_select(out=ident[:, :], in_=ones[:, :], compare_op=ALU.is_equal, fill=0.0, base=0, pattern=[[1, P]], channel_multiplier=-1)
            g_.affine_select(out=low, in_=ones[:, :], compare_op=ALU.is_gt, fill=0.0, base=0,
                             pattern=[[-1, P]], channel_multiplier=1).then_inc(s_cst, 1)

            pool.wait_ge(s_init, 16)
            for s in range(NU):
                def scatter(it, r):
                    n = 17 * s + it + 1
                    pool.wait_ge(s_pay, n)
                    pool.sem_inc(s_scrap, 1)
                    pool.wait_ge(s_pos, n)
                    pool.sem_inc(s_scrap, 1)
                    for a_ in range(NGS[s]):
                        g_.indirect_dma_start(out=Td[:, :], out_offset=bass.IndirectOffsetOnAxis(ap=POS[r][:, a_:a_ + 1], axis=0),
                                              in_=PST[r][:, a_, :], in_offset=None, bounds_check=NU * NB * SLOTS - 1,
                                              oob_is_err=False).then_inc(s_sct[r], 16)

                iterations(pool, scatter)
            read_flag(pool, "pool")

            def general(p):
                pool.wait_ge(s_tab[p], 32)

                def tile(g, j, t, n):
                    pool.wait_ge(s_stage, NT * PASSES.index(p) + t + 1)
                    pool.sem_inc(s_scrap, 1)
                    g_.indirect_dma_start(out=msg, out_offset=None, in_=Hd[:, :],
                                          in_offset=bass.IndirectOffsetOnAxis(ap=si[:, 0:1], axis=0)).then_inc(s_g[p], 16)
                    g_.indirect_dma_start(out=old, out_offset=None, in_=Gd[:, :],
                                          in_offset=bass.IndirectOffsetOnAxis(ap=di[:, 0:1], axis=0)).then_inc(s_old[p], 16)
                    pool.wait_ge(s_new, NT * PASSES.index(p) + t + 1)
                    pool.sem_inc(s_scrap, 1)
                    g_.indirect_dma_start(out=Gd[:, :], out_offset=bass.IndirectOffsetOnAxis(ap=xi[:, 0:1], axis=0),
                                          in_=new, in_offset=None, bounds_check=NP - 1,
                                          oob_is_err=False).then_inc(s_sc[p], 16)

                tiles(pool, tile)

            def source_factors():
                table = dinv_d.rearrange("(n o) -> n o", o=1)

                def gather(g, k):
                    g_.tensor_copy(sni[:, k, :], srcI[:, ds(g * J, J)])
                    pool.drain()
                    for j in range(J):
                        g_.indirect_dma_start(out=nsv[:, k, j:j + 1], out_offset=None, in_=table,
                                              in_offset=bass.IndirectOffsetOnAxis(ap=sni[:, k, j:j + 1], axis=0)).then_inc(s_nsg[k], 16)

                def keep(g, k, uses):
                    pool.wait_ge(s_nsg[k], 16 * J * uses)
                    pool.sem_inc(s_scrap, 1)
                    g_.tensor_copy(NS[:, ds(g * J, J)], nsv[:, k, :]).then_inc(s_nsc, 1)

                gather(0, 0)
                with pool.Fori(0, NG // 2) as i:
                    gather(2 * i + 1, 1)
                    keep(2 * i, 0, i + 1)
                    gather(2 * i + 2, 0)
                    keep(2 * i + 1, 1, i + 1)
                keep(NG - 1, 0, NG // 2 + 1)

            with pool.If(flags["pool"]):
                for p in PASSES:
                    general(p)
            with pool.Else():
                pool.wait_ge(s_dv, 32)
                source_factors()

        @block.vector
        def _(dve):
            v = nc.vector

            def three(ap):
                return ap.rearrange("p (b f) -> p b f", f=P)

            dve.wait_ge(s_idx, 64)
            dve.wait_ge(s_cst, 1)
            v.tensor_scalar(TI, srcI[:, :], 7, None, ALU.logical_shift_right)
            v.tensor_copy(dstF[:, :], dstI[:, :])
            dve.drain()
            v.tensor_copy(SB, TI)
            dve.drain()
            v.tensor_scalar(TI, srcI[:, :], P - 1, None, ALU.bitwise_and)
            dve.drain()
            v.tensor_copy(PAY[:, :, 0], TI)
            dve.drain()
            v.tensor_scalar(TI, dstI[:, :], 6, None, ALU.logical_shift_right)
            dve.drain()
            v.tensor_scalar(TF, TI, 1.0 / 7.0, 0.5 / 7.0 - 0.5, ALU.mult, ALU.add)
            dve.drain()
            v.tensor_scalar(UU, TF, 12582912.0, -12582912.0, ALU.add, ALU.add)
            dve.drain()
            v.scalar_tensor_tensor(out=PAY[:, :, 1], in0=UU, scalar=-float(UN), in1=dstF[:, :], op0=ALU.mult, op1=ALU.add)
            v.scalar_tensor_tensor(out=BASE, in0=UU, scalar=float(NB), in1=SB, op0=ALU.mult, op1=ALU.add)
            v.tensor_tensor(TF, UU, TG, ALU.subtract)
            dve.drain()
            v.tensor_scalar(BASE, BASE, float(SLOTS), None, ALU.mult)
            v.scalar_tensor_tensor(out=KEY, in0=TF, scalar=64.0, in1=SB, op0=ALU.mult, op1=ALU.add)
            dve.drain()
            end = slice((NG - 1) * J, NT)
            v.scalar_tensor_tensor(out=KEY[:, end], in0=KEY[:, end], scalar=1.0, in1=valid[:, :], op0=ALU.add, op1=ALU.mult)
            v.scalar_tensor_tensor(out=BASE[:, end], in0=BASE[:, end], scalar=-FAR, in1=valid[:, :], op0=ALU.add, op1=ALU.mult)
            dve.drain()
            v.tensor_scalar(KEY[:, end], KEY[:, end], -1.0, None, ALU.add)
            v.tensor_scalar(BASE[:, end], BASE[:, end], FAR, None, ALU.add).then_inc(s_key, 1)
            dve.drain()

            def measure(p):
                n, (lane, line, one, spread) = CU[p]
                v.tensor_reduce(mx[:, :], MX[:, :], axis=AX, op=ALU.max).then_inc(lane, 1)
                dve.wait_ge(line, n + 1)
                v.tensor_reduce(m1[:, :], CH[0:1, 0:P], axis=AX, op=ALU.max).then_inc(one, 1)
                dve.wait_ge(spread, n + 1)
                v.tensor_scalar(mc[:, :], CH[:, P:P + 1], 1e-30, None, ALU.max)
                dve.drain()
                v.tensor_scalar(me[:, :], mc[:, :].bitcast(i32), 0x7F800000, None, ALU.bitwise_and)
                dve.drain()
                v.tensor_scalar(SC[:, p, 0:1].bitcast(i32), me[:, :], -1.0, float((254 + CENTRE) << 23), ALU.mult, ALU.add)
                v.tensor_scalar(SC[:, p, 1:2].bitcast(i32), me[:, :], float(-(CENTRE << 23)), None, ALU.add)
                dve.drain()

            def split(p, source):
                dve.drain().then_inc(s_scale, 1)
                with dve.Fori(0, NQ) as q:
                    cols = ds(q * QN, QN)
                    dve.wait_ge(s_hi, 7 * p + q + 1)
                    v.scalar_tensor_tensor(out=LO[:, cols], in0=source[:, cols], scalar=SC[:, p, 0:1], in1=HI[:, cols],
                                           op0=ALU.mult, op1=ALU.subtract).then_inc(s_split, 1)

            def prelude():
                dve.wait_ge(s_wt, 1)
                v.tensor_copy(WT[:, :, :].rearrange("p k f -> p (k f)"), WTP)
                dve.wait_ge(s_x, 32)
                for q in range(NQ):
                    v.tensor_reduce(MX[:, q:q + 1], XN[:, q * QN:(q + 1) * QN], axis=AX, op=ALU.max, apply_absolute_value=True)
                dve.drain()
                measure(0)
                split(0, XN)

            for s in range(NU + LAG):
                u = s - LAG
                if s == 1:
                    prelude()
                def indicators(m, k_):
                    n = NB * u + m
                    if isinstance(m, int) and m == 0:
                        if n:
                            dve.wait_ge(s_bm, n)
                    elif not (isinstance(n, int) and n <= 2):
                        dve.wait_ge(s_bm, n - 2)
                    for k in range(3 if isinstance(m, int) and m < 4 else 2):
                        v.tensor_scalar(OHS[k_][k], iot[:, 0:P], SLD[u % 2][:, 2 * k, ds(m, 1)], None, ALU.is_equal)
                        last = v.tensor_scalar(OHD[k_][k], iot[:, :], SLD[u % 2][:, 2 * k + 1, ds(m, 1)], None, ALU.is_equal)
                    last.then_inc(s_ohb, 1)

                def positions(it, r, ng):
                    dve.wait_ge(s_rk, G0[s] * J + (it + 1) * ng)
                    dve.sem_inc(s_scrap, 1)
                    if s or not isinstance(it, int) or it >= SR:
                        dve.wait_ge(s_sct[r], scattered(s, r, it))
                        dve.sem_inc(s_scrap, 1)
                    cols = slice(G0[s], G0[s] + ng)
                    v.tensor_tensor(POS[r][:, 0:ng].unsqueeze(2),
                                    RK.rearrange("p (g j) -> p g j", j=J)[:, cols, ds(it, 1)],
                                    BASE.rearrange("p (g j) -> p g j", j=J)[:, cols, ds(it, 1)], ALU.add).then_inc(s_pos, 1)

                def step(it, r):
                    b = r % 2
                    ng = NGS[s] if s < NU else 0
                    nb = builds(it) if u >= 0 else 0
                    n0 = G0[min(s, NU)] * J + it * ng

                    def hot(a_):
                        v.tensor_scalar(OHK[b][a_], iok[:, :, :].rearrange("p a c -> p (a c)"), KEY[:, ds((G0[s] + a_) * J + it, 1)], None,
                                        ALU.is_equal).then_inc(s_oh, 1)

                    if ng:
                        hot(0)
                    for a_ in range(max(ng, nb)):
                        if a_ + 1 < ng:
                            hot(a_ + 1)
                        if a_ < nb and nb == 3:
                            indicators(3 * it + a_ + 1, (a_ + 1) % 3)
                        if a_ == 0 and ng and not (isinstance(it, int) and it == 0):
                            positions(it - 1, (r - 1) % SR, ng)
                        if a_ < ng:
                            dve.wait_ge(s_rp, n0 + a_ + 1)
                            t = ds((G0[s] + a_) * J + it, 1)
                            v.scalar_tensor_tensor(out=JK[a_].rearrange("p (a c) -> p a c", a=2), in0=iok[:, :, :], scalar=KEY[:, t],
                                                   in1=RP[:, 64 * s:64 * s + 128].rearrange("p (a c) -> p a c", a=2)[:, :, 0:NB],
                                                   op0=ALU.is_equal, op1=ALU.mult, accum_out=RK[:, t]).then_inc(s_rk, 1)
                    if ng and isinstance(it, int) and it == J - 1:
                        positions(it, r, ng)

                if u >= 0:
                    dve.wait_ge(s_sld, u + 1)
                    indicators(0, 0)
                iterations(dve, step)

            dve.drain()
            v.tensor_scalar(TF, SB, float(P), None, ALU.mult)
            dve.drain()
            v.scalar_tensor_tensor(out=TF, in0=UU, scalar=-float(UN), in1=TF, op0=ALU.mult, op1=ALU.add)
            dve.drain()
            v.tensor_scalar(CAP, TF, -float(P), float(P), ALU.is_gt, ALU.mult)
            dve.drain()
            v.scalar_tensor_tensor(out=CAP, in0=TF, scalar=float(UN), in1=CAP, op0=ALU.is_lt, op1=ALU.mult)
            dve.drain()
            v.tensor_tensor(RK, RK, CAP, ALU.subtract)
            g3 = [P, NG, J]
            dve.drain()
            v.tensor_scalar(RK, RK, 2.0 * P, None, ALU.is_ge)
            v.tensor_tensor(dstF[:, :].rearrange("p (g j) -> p g j", j=J), dstF[:, :].rearrange("p (g j) -> p g j", j=J),
                            gwin[:, :].unsqueeze(2).to_broadcast(g3), ALU.subtract)
            dve.drain()
            v.scalar_tensor_tensor(out=RK, in0=dstF[:, :], scalar=0.0, in1=RK, op0=ALU.is_lt, op1=ALU.max)
            dve.drain()
            v.scalar_tensor_tensor(out=RK, in0=dstF[:, :], scalar=float(WIN), in1=RK, op0=ALU.is_ge, op1=ALU.max)
            dve.drain()
            v.tensor_tensor(RK[:, end], RK[:, end], valid[:, :], ALU.mult)
            dve.drain()
            v.tensor_reduce(fl[:, 0:1], RK, axis=AX, op=ALU.max).then_inc(s_f1, 1)
            dve.wait_ge(s_f2, 1)
            v.tensor_scalar(flag[:, :], CH[:, 0:1], 0.5, None, ALU.is_gt).then_inc(s_flag, 1)
            read_flag(dve, "dve")

            def general(p):
                def tile(g, j, t, n):
                    m = NT * PASSES.index(p) + t + 1
                    v.tensor_copy(si[:, :], srcI[:, ds(t, 1)])
                    v.tensor_copy(di[:, :], dstI[:, ds(t, 1)])
                    v.tensor_scalar(Dg, ident[:, :], dstF[:, ds(t, 1)], None, ALU.mult).then_inc(s_stage, 1)
                    dve.wait_ge(s_bc, m)
                    v.tensor_scalar(M, PB, dstF[:, ds(t, 1)], None, ALU.is_equal)
                    dve.drain()
                    v.tensor_tensor_reduce(out=ML, in0=M, in1=low, scale=1.0, scalar=0.0,
                                           op0=ALU.mult, op1=ALU.add, accum_out=cl[:, :])
                    dve.drain()
                    v.tensor_scalar(far[:, :], cl[:, :], 0.5, FAR, ALU.is_gt, ALU.mult)
                    dve.drain()
                    dve.wait_ge(s_g[p], 16 * (t + 1))
                    if p == "attr":
                        v.tensor_tensor(xi[:, :], far[:, :], dstF[:, ds(t, 1)], ALU.add)
                        dve.wait_ge(s_attr, 16 * (t + 1))
                        v.tensor_tensor(msg, msg, at, ALU.mult).then_inc(s_m, 1)
                        dve.drain().then_inc(s_held, 1)
                    else:
                        v.tensor_tensor(xi[:, :], far[:, :], dstF[:, ds(t, 1)], ALU.add).then_inc(s_m, 1)
                    dve.wait_ge(s_cmb, m)
                    dve.sem_inc(s_scrap, 1)
                    dve.wait_ge(s_old[p], 16 * (t + 1))
                    v.tensor_tensor(new, PC, old, ALU.add).then_inc(s_new, 1)
                    dve.wait_ge(s_sc[p], 16 * (t + 1))
                    dve.sem_inc(s_scrap, 1)

                tiles(dve, tile)

            def general_sums(p, done, n):
                with dve.Fori(0, NQ) as q:
                    dve.wait_ge(s_ax, agu(p) + q + 1)
                    cols = ds(q * QN, QN)
                    if p in (1, 2, 3, 6, 7):
                        v.tensor_tensor(AT[:, cols], X[:, 0:QN], RB[:, cols], ALU.mult).then_inc(done, n)
                    else:
                        v.tensor_copy(AT[:, cols], X[:, 0:QN]).then_inc(done, n)
                    dve.drain().then_inc(s_axf, 1)

            with dve.If(flags["dve"]):
                v.tensor_copy(dstF[:, :], dstI[:, :])
                dve.drain()
                general("cnt")
            dve.wait_ge(s_cn, 32)
            v.tensor_scalar(c1[:, :], CN[:, :], 1.0, None, ALU.add).then_inc(s_sq, 1)
            v.tensor_scalar(c2[:, :], CN[:, :], 1.0, None, ALU.max)
            dve.wait_ge(s_sr, 1)
            v.reciprocal(dinv[:, :], SQ[:, :])
            dve.drain()
            v.reciprocal(idg[:, :], c1[:, :])
            v.reciprocal(rc[:, :], c2[:, :]).then_inc(s_deg, 1)
            v.tensor_copy(blk(HN), dinv[:, :].unsqueeze(2).to_broadcast([P, NB, P])).then_inc(s_deg, 1)
            dve.drain()
            with dve.If(flags["dve"]):
                dve.sem_inc(s_held, 1)
                general("attr")
                general(0)
                general_sums(0, s_at0, 1)

            def row(k):
                return BR[:, k, :].unsqueeze(1).to_broadcast([P, QB, P])

            def of(t, q):
                return t[:, ds(q * QB, QB)].unsqueeze(2).to_broadcast([P, QB, P])

            def norm(p, q):
                for b in range(QB):
                    v.bn_stats(ST[:, b, :], T1[:, b * P:(b + 1) * P])
                dve.drain()
                for b in range(QB):
                    v.bn_aggr(MV[:, b, :], ST[:, b, :])
                dve.drain()
                v.tensor_scalar(VE[:, :], MV[:, :, 1], EPS, None, ALU.add).then_inc(s_var, 1)
                dve.wait_ge(s_sd, LU[p] + q + 1)
                v.reciprocal(RS[:, :], SD[:, :])
                dve.drain()
                for b in range(QB):
                    last = v.tensor_scalar(XN[:, ds(q * QN + b * P, P)], T1[:, b * P:(b + 1) * P], MV[:, b, 0:1], RS[:, b:b + 1],
                                           ALU.subtract, ALU.mult)
                return last

            def y_full(n):
                dve.drain()
                dve.wait_ge(s_yf, n)

            def biggest(q):
                dve.drain()
                v.tensor_reduce(MX[:, ds(q, 1)], HN[:, ds(q * QN, QN)], axis=AX, op=ALU.max, apply_absolute_value=True)

            def after(p):
                with dve.Fori(0, NQ) as q:
                    cols = ds(q * QN, QN)
                    y_full(YU[p] + q + 1)
                    y = three(Y[:, 0:QN])
                    t1 = three(T1[:, :])
                    if p == 0:
                        v.tensor_tensor(t1, y, row(0), ALU.add).then_inc(s_yfree, 1)
                        dve.drain()
                        v.scalar_tensor_tensor(out=T1[:, :], in0=T1[:, :], scalar=0.0, in1=XN[:, cols], op0=ALU.max, op1=ALU.add)
                        dve.drain()
                        norm(p, q)
                        dve.drain()
                        v.tensor_tensor(three(HN[:, cols]), three(XN[:, cols]), of(dinv, q), ALU.mult).then_inc(s_h, 1)
                    elif p in (1, 2, 3):
                        v.tensor_tensor(three(HN[:, cols]), y, of(dinv, q), ALU.mult).then_inc(s_h, 1)
                        dve.drain().then_inc(s_yfree, 1)
                        biggest(q)
                    elif p == 4:
                        v.tensor_tensor(t1, y, of(dinv, q), ALU.mult).then_inc(s_yfree, 1)
                        dve.drain()
                        v.tensor_tensor(t1, t1, row(1), ALU.add)
                        dve.drain()
                        v.tensor_tensor(T1[:, :], T1[:, :], XN[:, cols], ALU.add)
                        dve.drain()
                        norm(p, q).then_inc(s_xn, 1)
                    elif p == 5:
                        v.tensor_tensor(t1, y, of(dinv, q), ALU.mult).then_inc(s_yfree, 1)
                        dve.drain()
                        v.tensor_tensor(T1[:, :], T1[:, :], XN[:, cols], ALU.add)
                        dve.drain()
                        v.tensor_tensor(T1[:, :], T1[:, :], HR[:, cols], ALU.add)
                        dve.drain()
                        norm(p, q).then_inc(s_xn, 1)
                        dve.drain().then_inc(s_h, 1)
                    elif p == 6:
                        v.tensor_tensor(t1, y, row(4), ALU.add).then_inc(s_yfree, 1)
                        dve.drain()
                        v.tensor_scalar(HN[:, cols], T1[:, :], 0.0, None, ALU.max).then_inc(s_h, 1)
                        biggest(q)
                    else:
                        v.tensor_tensor(t1, y, row(5), ALU.add).then_inc(s_yfree, 1)
                        dve.drain()
                        v.tensor_tensor(T1[:, :], T1[:, :], XN[:, cols], ALU.add)
                        dve.drain()
                        norm(p, q).then_inc(s_h, 1)
                if p == 4:
                    with dve.Fori(0, NQ) as q:
                        cols = ds(q * QN, QN)
                        y_full(YU[4] + 7 + q + 1)
                        v.tensor_tensor(three(T1[:, :]), three(Y[:, 0:QN]), row(2), ALU.add).then_inc(s_yfree, 1)
                        dve.drain()
                        v.tensor_tensor(three(HN[:, cols]), three(T1[:, :]), row(3), ALU.add)
                        v.tensor_tensor(three(HR[:, cols]), three(T1[:, :]), row(6), ALU.add)
                        dve.drain()
                        v.tensor_tensor(three(HR[:, cols]), three(HR[:, cols]), of(idg, q), ALU.mult)
                        v.tensor_tensor(three(HN[:, cols]), three(HN[:, cols]), of(dinv, q), ALU.mult).then_inc(s_h, 1)
                        biggest(q)
                dve.drain()
                if p + 1 in MEASURED:
                    measure(p + 1)
                if p < 7:
                    split(p + 1, XN if p == 5 else HN)

            def fast_sums(p):
                for h in range(2):
                    dve.wait_ge(s_agg, 2 * (p - 1) + h + 1)
                    for k in range(UH):
                        cols = slice((UH * h + k) * UN, (UH * h + k + 1) * UN)
                        if p in (1, 2, 3, 6, 7):
                            v.scalar_tensor_tensor(out=AT[:, cols], in0=AGB[k], scalar=SC[:, p, 1:2], in1=RB[:, cols],
                                                   op0=ALU.mult, op1=ALU.mult).then_inc(s_at, 1)
                        else:
                            v.tensor_scalar(AT[:, cols], AGB[k], SC[:, p, 1:2], None, ALU.mult).then_inc(s_at, 1)

            def edge_measure():
                def group(g, k, uses):
                    dve.wait_ge(s_ael[k], 16 * uses)
                    v.tensor_reduce(MXE[:, ds(g, 1)], AE[k], axis=AX, op=ALU.max, apply_absolute_value=True).then_inc(s_aem, 1)

                group(0, 0, 1)
                with dve.Fori(0, NG // 2) as i:
                    group(2 * i + 1, 1, i + 1)
                    group(2 * i + 2, 0, i + 2)
                dve.drain()
                v.tensor_reduce(MX[:, :], MXE.rearrange("p (q g) -> p q g", q=NQ), axis=AX, op=ALU.max)
                dve.drain()
                measure(EDGES)

            def edge_sums():
                v.memset(RBW[:, :], 0.0)
                dve.wait_ge(s_nsc, NG)
                dve.drain()

                def add(g, k):
                    dve.wait_ge(s_eam, g + 2)
                    win = RBW[:, ds(P * g, WIN)]
                    v.scalar_tensor_tensor(out=win, in0=CH[:, 0:WIN], scalar=SC[:, EDGES, 1:2], in1=win,
                                           op0=ALU.mult, op1=ALU.add).then_inc(s_eae, 1)

                def group(g, k, uses):
                    e3 = AE[k].rearrange("p (j f) -> p j f", j=J)
                    dve.wait_ge(s_ael[k], uses)
                    v.tensor_tensor(e3, e3, NS[:, ds(g * J, J)].unsqueeze(2).to_broadcast([P, J, DE]), ALU.mult).then_inc(s_aes, 1)
                    if not isinstance(g, int):
                        dve.wait_ge(s_eam, g)
                    for j in range(J):
                        v.tensor_scalar(OHW[k][:, j, :], iot[:, 0:WIN], dstF[:, ds(g * J + j, 1)], None, ALU.is_equal)
                    dve.wait_ge(s_ahi, g + 1)
                    v.scalar_tensor_tensor(out=AHL[k][:, :, DE:2 * DE], in0=e3, scalar=SC[:, EDGES, 0:1], in1=AHL[k][:, :, 0:DE],
                                           op0=ALU.mult, op1=ALU.subtract).then_inc(s_ahl, 1)

                at1 = 16 * (NG // 2)
                group(0, 0, at1 + 16 + 16)
                with dve.Fori(0, (NG - 1) // 4) as i:
                    for m in range(4):
                        g = 4 * i + 1 + m
                        k = (m + 1) % 2
                        group(g, k, (at1 if k else at1 + 16) + 32 * i + (16 * (m // 2 + 1) if k else 16 * ((m + 1) // 2 + 1)))
                        dve.drain()
                        add(g - 1, 1 - k)
                        dve.drain()
                add(NG - 1, 0)
                dve.drain()

            after(0)
            for p in range(1, 8):
                if p in (1, 6):
                    dve.wait_ge(s_rb, 16 if p == 1 else 32)
                with dve.If(flags["dve"]):
                    general(p)
                    general_sums(p, s_at, 2)
                with dve.Else():
                    if p == 1:
                        edge_measure()
                    if p == 4:
                        edge_sums()
                    fast_sums(p)
                after(p)

        @block.scalar
        def _(act):
            c = nc.scalar

            def high(p, source):
                act.wait_ge(s_scale, p + 1)
                with act.Fori(0, NQ) as q:
                    cols = ds(q * QN, QN)
                    c.activation(HI[:, cols], source[:, cols], ACT.Copy, scale=SC[:, p, 0:1]).then_inc(s_hi, 1)

            act.wait_ge(s_key, 1)
            for s in range(NU + LAG):
                u = s - LAG
                if s == 1:
                    high(0, XN)

                def step(it, r):
                    b = r % 2
                    if s < NU:
                        if s or not isinstance(it, int) or it >= SR:
                            act.wait_ge(s_sct[r], scattered(s, r, it))
                            act.sem_inc(s_scrap, 1)
                        ng = NGS[s]
                        c.copy(PST[r][:, 0:ng, :],
                               PAY.rearrange("p (g j) c -> p g j c", j=J)[:, G0[s]:G0[s] + ng, ds(it, 1), :].rearrange("p g o c -> p g (o c)")
                               ).then_inc(s_pay, 1)
                    if u < 0:
                        return
                    for a_ in range(builds(it)):
                        n = NB * u + 3 * it + a_
                        if isinstance(it, int) and 3 * it + a_ == 0:
                            if n:
                                act.wait_ge(s_spm, n)
                        elif not isinstance(n, int) or n > 5:
                            act.wait_ge(s_spm, n - 5)
                            act.sem_inc(s_scrap, 1)
                        use = u * (9 if (b, a_) == (0, 0) else 8)
                        if isinstance(it, int):
                            if use + it // 2:
                                act.wait_ge(s_aw[b][a_], 16 * (use + it // 2))
                        else:
                            act.wait_ge(s_aw[b][a_], 8 * (it - b) + 16 * use)
                            act.sem_inc(s_scrap, 1)
                        act.wait_ge(s_bm, n + 1)
                        c.copy(A16[b][a_], BP[a_]).then_inc(s_ev8, 1)

                iterations(act, step)
                if 1 <= s <= NU:
                    w = s - 1
                    if w >= 2:
                        act.wait_ge(s_ohb, NB * (w - 1))
                    act.wait_ge(s_tt, w + 1)
                    c.copy(SLD[w % 2], TP[:, 0:6 * 64].rearrange("p (k n) -> p k n", n=64)[:, :, 0:NB]).then_inc(s_sld, 1)
                if u >= 0:
                    cols = slice(UN * u, UN * (u + 1))
                    act.wait_ge(s_un, u + 1)
                    c.copy(RB[:, cols], CNT)
                    c.activation(AT[:, cols], AGG, ACT.Copy, scale=SC[:, 0, 1:2]).then_inc(s_at, 1)
            read_flag(act, "act")
            act.wait_ge(s_sq, 1)
            c.activation(SQ[:, :], c1[:, :], ACT.Sqrt).then_inc(s_sr, 1)

            def root(n):
                act.wait_ge(s_var, n)
                c.activation(SD[:, :], VE[:, :], ACT.Sqrt).then_inc(s_sd, 1)

            def edge_features(wait_for):
                def load(g, k):
                    full = not isinstance(g, int) or g < NG - 1
                    n = P if full else PTAIL
                    act.dma_start(AE[k][0:n, :], a["edge_attr_64"][ds(g * GE, GE) if full else slice(g * GE, E), :]
                                  .rearrange("(p j) f -> p (j f)", j=J)).then_inc(s_ael[k], 16)

                return load

            for p in range(8):
                if p == 4:
                    with act.If(flags["act"]):
                        with act.Fori(0, NQ) as q:
                            act.wait_ge(s_ax, agu(4) - 7 + q + 1)
                            c.copy(RB[:, ds(q * QN, QN)], X[:, 0:QN])
                            act.drain().then_inc(s_axf, 1)
                    with act.Else():
                        load = edge_features(None)
                        act.wait_ge(s_yf, YU[3] + 7)
                        load(0, 0)
                        load(1, 1)

                        def highs(g, k):
                            if not (isinstance(g, int) and g == 0):
                                act.wait_ge(s_eam, g)
                                act.sem_inc(s_scrap, 1)
                            act.wait_ge(s_aes, g + 1)
                            c.activation(AHL[k][:, :, 0:DE], AE[k].rearrange("p (j f) -> p j f", j=J), ACT.Copy,
                                         scale=SC[:, EDGES, 0:1]).then_inc(s_ahi, 1)

                        def refill(g, k):
                            act.wait_ge(s_ahl, g - 1)
                            load(g, k)

                        highs(0, 0)
                        refill(2, 0)
                        with act.Fori(0, (NG - 1) // 4 - 1) as i:
                            for m in range(4):
                                highs(4 * i + 1 + m, (m + 1) % 2)
                                refill(4 * i + 3 + m, (m + 1) % 2)
                        for g in range(NG - 4, NG):
                            highs(g, g % 2)
                            if g + 2 < NG:
                                refill(g + 2, g % 2)
                if p == 1:
                    with act.If(flags["act"]):
                        act.sem_inc(s_scrap, 1)
                    with act.Else():
                        load = edge_features(None)
                        act.wait_ge(s_yf, YU[0] + 7)
                        load(0, 0)
                        load(1, 1)
                        with act.Fori(1, NG // 2) as i:
                            for k in range(2):
                                act.wait_ge(s_aem, 2 * i + k - 1)
                                load(2 * i + k, k)
                        act.wait_ge(s_aem, NG - 2)
                        load(NG - 1, 0)
                if p in (0, 1):
                    with act.Fori(0, NQ) as q:
                        act.wait_ge(s_xf, XU[p] + q + 1)
                        for h in range(2):
                            c.activation(TB[:, ds(q * QN + h * UN, UN)], X[:, 512 * h:512 * h + UN], ACT.Relu, bias=BC[:, p:p + 1])
                        act.drain().then_inc(s_tb, 1)
                        act.sem_inc(s_xfree, 1)
                        if p == 0:
                            root(LU[p] + q + 1)
                elif p in (2, 3):
                    with act.Fori(0, NQ) as q:
                        act.wait_ge(s_at, atu(p) + 2 * q + 2)
                        cols = ds(q * QN, QN)
                        c.activation(TB[:, cols], AT[:, cols], ACT.Relu, bias=BC[:, p:p + 1]).then_inc(s_tb, 1)
                elif p in (4, 5, 6):
                    with act.Fori(0, NQ) as q:
                        if p < 6:
                            root(LU[p] + q + 1)
                        act.wait_ge(s_zf, ZU[p] + q + 1)
                        c.copy(TB[:, ds(q * QN, QN)], Z[:, 0:QN])
                        act.drain().then_inc(s_tb, 1)
                        act.sem_inc(s_zfree, 1)
                else:
                    with act.Fori(0, NQ) as q:
                        root(LU[p] + q + 1)
                if p < 7:
                    high(p + 1, XN if p == 5 else HN)

        @block.tensor
        def _(pe):
            t_ = nc.tensor

            def mm(out_, w, m, start=False):
                return t_.matmul(out_, w, m, start=start, stop=True, skip_group_check=True)

            pe.wait_ge(s_cst, 1)
            z16 = zeros[:, :].bitcast(f16)[:, 0:P]
            for k in range(2):
                mm(PS[:, 512 * k:512 * k + UN], z16, iot[:, :], start=True)
                mm(PS[:, 512 * k + UN:512 * k + 512], z16, iot[:, 0:512 - UN])
            for e in [s_xfree, s_yfree, s_zfree, s_axf, s_eam, s_eae] + s_af:
                pe.sem_inc(e, 1)

            def measured(p):
                n, (lane, line, one, spread) = CU[p]
                pe.wait_ge(lane, n + 1)
                t_.matmul(CH[0:1, 0:P], mx[:, 0:1], ident[:, :], start=True, stop=True).then_inc(line, 1)
                pe.wait_ge(one, n + 1)
                t_.matmul(CH[:, P:P + 1], ones[0:1, :], m1[0:1, 0:1], start=True, stop=True).then_inc(spread, 1)

            for s in range(NU + LAG):
                u = s - LAG
                if s == 1:
                    pe.wait_ge(s_w, 16 * 24)
                    for k in range(6):
                        last = t_.transpose(WTP[:, k * P:(k + 1) * P], WR[:, k, :], ident[:, :])
                    last.then_inc(s_wt, 1)
                    measured(0)
                if u == 0:
                    pe.wait_ge(s_split, NQ)

                def used(n, b, a_, first):
                    k = (n + DLO[u]) % NB
                    cols = ds(k * P, P) if not isinstance(k, int) else slice(k * P, k * P + P)
                    mm(AGG, HI[:, cols], A16[b][a_], start=first)
                    mm(AGG, LO[:, cols], A16[b][a_])
                    mm(CNT, O16[:, :], A16[b][a_], start=first).then_inc(s_spm, 1)

                def step(it, r):
                    b = r % 2
                    ng = NGS[s] if s < NU else 0
                    nb = builds(it) if u >= 0 else 0
                    for a_ in range(max(ng, nb)):
                        t = G0[min(s, NU)] * J + it * ng + a_
                        both = range(2 if s + 1 < NU else 1)
                        if a_ < ng:
                            pe.wait_ge(s_oh, t + 1)
                            for k in both:
                                last = mm(RP[:, 64 * (s + k):64 * (s + k) + NB], Lt[:, :], OHK[b][a_][:, NB * k:NB * k + NB])
                            last.then_inc(s_rp, 1)
                        if a_ < nb:
                            n = 3 * it + a_
                            N_ = NB * u + n
                            first = isinstance(n, int) and n == 0
                            pe.wait_ge(s_ohb, N_ + 1)
                            if not (isinstance(N_, int) and N_ < 3):
                                pe.wait_ge(s_ev8, N_ if first else N_ - 2)
                            for k in range(slots_of(it, a_)):
                                last = mm(BP[a_], OHS[a_][k], OHD[a_][k], start=k == 0)
                            last.then_inc(s_bm, 1)
                            if not first:
                                if isinstance(n, int) and n == 1 and u:
                                    pe.wait_ge(s_at, u)
                                pe.wait_ge(s_ev8, N_)
                                used(n - 1, b if a_ else 1 - b, (a_ - 1) % 3, isinstance(n, int) and n == 1)
                        if a_ < ng:
                            pe.wait_ge(s_rk, t + 1)
                            for k in both:
                                mm(RP[:, 64 * (s + k):64 * (s + k) + NB], Uc[:, :], OHK[b][a_][:, NB * k:NB * k + NB])

                iterations(pe, step)
                if 1 <= s <= NU:
                    w = s - 1
                    pe.wait_ge(s_tabl[w % 2], 16 * sum(2 if DLO[x] else 1 for x in range(w % 2, w + 1, 2)))
                    if w:
                        pe.wait_ge(s_sld, w)
                    tab = TAB[w % 2].rearrange("p (r c) -> p r c", c=2)
                    for k in range(3):
                        for c in range(2):
                            q = 64 * (2 * k + c)
                            last = t_.transpose(TP[:, q:q + NB], tab[0:NB, P * k:P * (k + 1), c], I16[0:NB, 0:NB])
                    last.then_inc(s_tt, 1)
                if u >= 0:
                    pe.wait_ge(s_ev8, NB * (u + 1))
                    used(NB - 1, 0, 0, False)
                    for blk_, c0, d0, w_ in ahead(u):
                        for part in (HI, LO):
                            mm(AGG[:, d0:d0 + w_], part[:, blk_ * P:(blk_ + 1) * P], I16[:, c0:c0 + w_])
                    pe.drain().then_inc(s_un, 1)
            pe.wait_ge(s_f1, 1)
            t_.matmul(CH[:, 0:1], ones[:, :], fl[:, 0:1], start=True, stop=True).then_inc(s_f2, 1)
            read_flag(pe, "pe")

            def general(p):
                def tile(g, j, t, n):
                    m = NT * PASSES.index(p) + t + 1
                    pe.wait_ge(s_stage, m)
                    t_.matmul(PB, ones[:, :], Dg, start=True, stop=True).then_inc(s_bc, 1)
                    pe.wait_ge(s_m, m)
                    t_.matmul(PC, M, msg, start=True, stop=True).then_inc(s_cmb, 1)

                tiles(pe, tile)

            def sums(n, loaded):
                pe.wait_ge(s_agn, 16 * loaded)
                for q in range(NQ):
                    pe.wait_ge(s_axf, n + q + 1)
                    for b in range(QB):
                        last = t_.transpose(X[:, b * P:(b + 1) * P], AGN[:, ds(q * QN + b * P, P)], ident[:, :])
                    last.then_inc(s_ax, 1)

            def node_stage(n, q, parts):
                pe.wait_ge(s_yfree, n + q + 1)
                for b in range(QB):
                    for k, (t, w) in enumerate(parts):
                        last = t_.matmul(Y[:, b * P:(b + 1) * P], t[:, ds(q * QN + b * P, P)], w,
                                         start=k == 0, stop=k == len(parts) - 1)
                last.then_inc(s_yf, 1)

            def turn(p, q, source):
                pe.wait_ge(s_zfree, ZU[p] + q + 1)
                for b in range(QB):
                    last = t_.transpose(Z[:, b * P:(b + 1) * P], source[:, ds(q * QN + b * P, P)], ident[:, :])
                last.then_inc(s_zf, 1)

            def edge_group(g, k):
                pe.wait_ge(s_ahl, g + 1)
                if not (isinstance(g, int) and g == 0):
                    pe.wait_ge(s_eae, g + 1)
                for j in range(J):
                    last = mm(CH[:, 0:WIN], AHL[k][:, j, :], OHW[k][:, j, :], start=j == 0)
                last.then_inc(s_eam, 1)

            def fast(p):
                slot = ring(p)
                pe.wait_ge(s_tb, TU[p - 1] + 7)
                pe.wait_ge(s_split, 7 * p + 7)
                for h in range(2):
                    n = 2 * (p - 1) + h

                    def block_(k, m, use, first=False):
                        pe.wait_ge(s_al[m], 16 * use)
                        cols = ds(k * P, P) if not isinstance(k, int) else slice(k * P, k * P + P)
                        for part in (HI, LO):
                            for j in range(UH):
                                if first and part is HI and h:
                                    pe.wait_ge(s_at, atu(p) + j + 1)
                                last = mm(AGB[j], part[:, cols], slot[m][:, UN * j:UN * (j + 1)], start=first and part is HI)
                        last.then_inc(s_af[m], 1)

                    block_(0, RING, n + 1, True)
                    if p == 4 and h == 0:
                        edge_group(0, 0)
                    with pe.Fori(0, (NB - 1) // RING) as i:
                        for m in range(RING):
                            block_(RING * i + 1 + m, m, 12 * n + i + 1)
                            if p == 4 and h == 0:
                                edge_group(RING * i + 1 + m, (m + 1) % 2)
                    if p in SELF:
                        for j in range(UH):
                            for blk_, c0, d0, w_ in ahead(UH * h + j):
                                for part in (HI, LO):
                                    mm(AGB[j][:, d0:d0 + w_], part[:, blk_ * P:(blk_ + 1) * P], I16[:, c0:c0 + w_])
                    pe.drain().then_inc(s_agg, 1)
                    if p == 1 and h == 0:
                        measured(EDGES)

            with pe.If(flags["pe"]):
                pe.wait_ge(s_at, NU)
                general("cnt")
                general("attr")
                general(0)
                sums(agu(0), 1)
                pe.wait_ge(s_at0, NQ)
            for p in range(8):
                if p:
                    with pe.If(flags["pe"]):
                        general(p)
                        if p == 4:
                            sums(agu(4) - 7, 5)
                        sums(agu(p), p + 1 + (p >= 4))
                    with pe.Else():
                        fast(p)
                pe.wait_ge(s_at, atu(p + 1))
                if p in (0, 1):
                    w = WT[:, 0, :] if p == 0 else WN[:, 0, :]
                    for q in range(NQ):
                        pe.wait_ge(s_xfree, XU[p] + q + 1)
                        for h in range(2):
                            last = t_.matmul(X[:, 512 * h:512 * h + UN], w, AT[:, ds(q * QN + h * UN, UN)], start=True, stop=True)
                        last.then_inc(s_xf, 1)
                        pe.wait_ge(s_tb, TU[p] + q + 1)
                        node_stage(YU[p], q, [(TB, WT[:, 1, :] if p == 0 else WN[:, 1, :])])
                elif p in (2, 3):
                    for q in range(NQ):
                        pe.wait_ge(s_tb, TU[p] + q + 1)
                        node_stage(YU[p], q, [(TB, WN[:, p, :])])
                elif p == 4:
                    for q in range(NQ):
                        node_stage(YU[p], q, [(AT, ident[:, :])])
                        pe.wait_ge(s_xn, q + 1)
                        turn(p, q, XN)
                    for q in range(NQ):
                        pe.wait_ge(s_tb, TU[p] + q + 1)
                        node_stage(YU[p] + 7, q, [(TB, WN[:, 4, :])])
                elif p == 5:
                    for q in range(NQ):
                        node_stage(YU[p], q, [(AT, ident[:, :]), (RB, We2[:, :])])
                        pe.wait_ge(s_xn, 7 + q + 1)
                        turn(p, q, XN)
                elif p == 6:
                    pe.wait_ge(s_tb, TU[6])
                    for q in range(NQ):
                        node_stage(YU[p], q, [(AT, WT[:, 2, :]), (TB, WT[:, 3, :])])
                        pe.wait_ge(s_h, 7 * 6 + q + 1)
                        turn(p, q, HN)
                else:
                    pe.wait_ge(s_tb, TU[6] + 7)
                    for q in range(NQ):
                        node_stage(YU[p], q, [(AT, WT[:, 4, :]), (TB, WT[:, 5, :])])
                if p + 1 in MEASURED:
                    measured(p + 1)


_INS = ['x', 'src', 'dst', 'edge_attr_64', 'L0_gnn_W1', 'L0_gnn_b1', 'L0_gnn_W2', 'L0_gnn_b2', 'L1_gnn_W1', 'L1_gnn_b1',
        'L1_gnn_W2', 'L1_gnn_b2', 'L1_gnn_W3', 'L1_gnn_b3', 'L1_gnn_W4', 'L1_gnn_b4', 'L2_gnn_Wn', 'L2_gnn_bn',
        'L2_gnn_We', 'L2_gnn_be', 'L2_gnn_resid', 'L3_gnn_W_l0', 'L3_gnn_b_l0', 'L3_gnn_W_r0', 'L3_gnn_W_l1',
        'L3_gnn_b_l1', 'L3_gnn_W_r1']


def kernel(**inputs):
    import numpy as _np
    import concourse.bacc as _bacc
    from concourse import mybir as _mybir
    from concourse.bass_utils import run_bass_kernel_spmd as _run

    nc = _bacc.Bacc("TRN2", target_bir_lowering=False, num_devices=1)
    arrays, aps = {}, {}
    for name in _INS:
        v = _np.ascontiguousarray(inputs[name])
        arrays[f"in_{name}_dram"] = v
        aps[name] = nc.dram_tensor(f"in_{name}_dram", v.shape, _mybir.dt.from_np(v.dtype), kind="ExternalInput").ap()
    out = nc.dram_tensor("out_0_dram", inputs["x"].shape, _mybir.dt.float32, kind="ExternalOutput").ap()
    build(nc, aps, out)
    r = _run(nc, [arrays], core_ids=[0])
    return r.results[0]["out_0_dram"]
```

```python
import concourse.bass as bass
from concourse import mybir
from contextlib import ExitStack

P = 128


def build(nc, a, out):
    fp32 = mybir.dt.float32
    i32 = mybir.dt.int32
    f16 = mybir.dt.float16
    ALU = mybir.AluOpType
    ACT = mybir.ActivationFunctionType
    AX = mybir.AxisListType.X
    ds = bass.ds

    N, D = a["x"].shape
    E, DE = a["edge_attr_64"].shape
    NB = -(-N // P)
    NP = NB * P
    NTAIL = N - (NB - 1) * P
    J = 17
    GE = P * J
    NG = -(-E // GE)
    PTAIL = (E - (NG - 1) * GE) // J
    assert PTAIL * J == E - (NG - 1) * GE
    NT = NG * J
    PADNODE = NP - 1
    QB = 7
    NQ = NB // QB
    QN = QB * P
    UN = QN // 2
    EPS = 1e-5
    FAR = 1.0e6

    NU = NP // UN
    UH = NU // 2
    SLOTS = 3 * P
    WIN = 256
    MARGIN = 64
    LAG = 2
    G0 = [next(g for g in range(NG + 1) if g == NG or (P * g - MARGIN) // UN >= s) for s in range(NU + 1)]
    G0[0] = 0
    DLO = [UN * u // P for u in range(NU)]
    CENTRE = 14
    RING = 4
    SR = 4

    Hd = nc.dram_tensor("h_rows", (NP, D), fp32).ap()
    Gd = nc.dram_tensor("sum_rows", (NP, D), fp32).ap()
    Ed = nc.dram_tensor("attr_rows", (NP, D), fp32).ap()
    dinv_d = nc.dram_tensor("dinv_vec", (NP,), fp32).ap()
    rc_d = nc.dram_tensor("rc_vec", (NP,), fp32).ap()
    cnt_d = nc.dram_tensor("cnt_vec", (NP,), fp32).ap()
    Td = nc.dram_tensor("edge_table", (NU * NB * SLOTS, 2), f16).ap()
    Ad = nc.dram_tensor("adjacency", (2, NB, P, UH * UN), f16).ap()

    PASSES = ["cnt", "attr"] + list(range(8))
    SELF = [0, 1, 2, 3, 4]

    with ExitStack() as ctx:
        def sb(name, shape, dt=fp32):
            return ctx.enter_context(nc.sbuf_tensor(name, shape, dt))

        def sem(name):
            return ctx.enter_context(nc.semaphore(name))

        XN = sb("XN", [P, NP])
        HN = sb("HN", [P, NP])
        HR = sb("HR", [P, NP])
        AGN = sb("AGN", [P, NP])
        AT = sb("AT", [P, NP])
        TB = sb("TB", [P, NP])
        RBW = sb("RBW", [P, NP + 2 * MARGIN])
        RB = RBW[:, MARGIN:MARGIN + NP]
        S5 = sb("S5", [P, UH * UN // 2])
        ST = sb("ST", [P, NB, 6])
        MV = sb("MV", [P, NB, 2])
        VE = sb("VE", [P, NB])
        SD = sb("SD", [P, NB])
        RS = sb("RS", [P, NB])
        srcI = sb("srcI", [P, NT], i32)
        dstI = sb("dstI", [P, NT], i32)
        dstF = sb("dstF", [P, NT])
        ident = sb("ident", [P, P])
        ones = sb("ones", [P, P])
        zeros = sb("zeros", [P, P])
        WR = AT[:, 0:6 * P].rearrange("p (k f) -> p k f", k=6)
        WT = sb("WT", [P, 6, P])
        WN = sb("WN", [P, 5, P])
        We2 = sb("We2", [P, P])
        BC = sb("BC", [P, 4])
        BR = sb("BR", [P, 7, P])
        CN = sb("CN", [P, NB])
        dinv = sb("dinv", [P, NB])
        rc = sb("rc", [P, NB])
        idg = sb("idg", [P, NB])
        c1 = sb("c1", [P, NB])
        c2 = sb("c2", [P, NB])
        SQ = sb("SQ", [P, NB])
        si = sb("si", [P, 1], i32)
        di = sb("di", [P, 1], i32)
        xi = sb("xi", [P, 1], i32)
        Dg, M, ML, msg, old, new, at, low = (S5[:, k * P:(k + 1) * P] for k in range(8))
        cl = sb("cl", [P, 1])
        far = sb("far", [P, 1])
        HI = AGN[:, 0:NP // 2].bitcast(f16)
        LO = AGN[:, NP // 2:NP].bitcast(f16)
        MX = sb("MX", [P, NQ])
        mx = sb("mx", [P, 1])
        m1 = sb("m1", [1, 1])
        mc = sb("mc", [P, 1])
        me = sb("me", [P, 1], i32)
        SC = sb("SC", [P, 9, 2])
        iot = sb("iot", [P, UN], f16)
        iok = sb("iok", [P, 2, NB], f16)
        Lt = sb("Lt", [P, P], f16)
        Uc = sb("Uc", [P, P], f16)
        I16 = sb("I16", [P, P], f16)
        O16 = sb("O16", [P, P], f16)
        valid = sb("valid", [P, J])
        fl = sb("fl", [P, 4])
        flag = sb("flag", [P, 1], i32)
        gwin = sb("gwin", [P, NG])
        MXE = sb("MXE", [P, NG])
        NS = dstI[:, :].bitcast(fp32)
        sni = sb("sni", [P, 2, J], i32)
        nsv = sb("nsv", [P, 2, J])
        KEY, BASE, RK, CAP, PAYW, UU, SB = (HR[:, k * NT:(k + 1) * NT] for k in range(7))
        KEY16 = HR[:, 7 * NT:7 * NT + (NT + 1) // 2].bitcast(f16)[:, 0:NT]
        PAY = PAYW.bitcast(f16).rearrange("p (t c) -> p t c", c=2)
        off = [0]

        def carve(cols, dt=f16):
            w = cols // (2 if dt == f16 else 1)
            v = TB[:, off[0]:off[0] + w]
            off[0] += w
            return v.bitcast(f16) if dt == f16 else (v.bitcast(dt) if dt != fp32 else v)

        OHK = [carve(4 * 2 * NB).rearrange("p (a c) -> p a c", a=4) for _ in range(2)]
        OHS = [carve(3 * P).rearrange("p (k c) -> p k c", k=3) for _ in range(3)]
        OHD = [[carve(UN) for _ in range(3)] for _ in range(3)]
        A16 = [[carve(UN) for _ in range(3)] for _ in range(2)]
        TAB = [carve(2 * SLOTS) for _ in range(2)]
        SLD = [carve(6 * NB, dt=fp32).rearrange("p (k n) -> p k n", n=NB) for _ in range(2)]
        S16 = [carve(3 * NB + 1)[:, 0:3 * NB].rearrange("p (k n) -> p k n", n=NB) for _ in range(2)]
        JK = [carve(2 * NB) for _ in range(4)]
        POS = [carve(4, dt=i32) for _ in range(SR)]
        PST = [carve(8).rearrange("p (a c) -> p a c", c=2) for _ in range(SR)]
        TI = HN[:, 0:NT].bitcast(i32)
        TF = HN[:, NT:2 * NT]
        TG = HN[:, 2 * NT:3 * NT]
        FILL = HN[:, 3 * NT:3 * NT + NU * NB * SLOTS // P].bitcast(f16)
        AE = [TB[:, k * J * DE:(k + 1) * J * DE] for k in range(2)]
        AHL = [HN[:, k * J * DE:(k + 1) * J * DE].bitcast(f16).rearrange("p (j f) -> p j f", j=J) for k in range(2)]
        OHW = [HN[:, (k + 1) * J * P:(k + 2) * J * P].bitcast(f16).rearrange("p (j f) -> p j f", j=J) for k in range(1)]
        OHW.append(TB[:, J * P:2 * J * P].bitcast(f16).rearrange("p (j f) -> p j f", j=J))

        PS = ctx.enter_context(nc.psum_tensor("PS", [P, 4096], fp32))
        RP = PS[:, 0:1024]
        BP = [PS[:, 512 * (2 + k):512 * (2 + k) + UN] for k in range(3)]
        AGG, CNT = PS[:, 2560:2560 + UN], PS[:, 3072:3072 + UN]
        TP = PS[:, 3584:4096].bitcast(f16)
        CH = PS[:, 3584:4096]
        WTP = PS[:, 2560:2560 + 6 * P]
        AGB = [PS[:, 512 * k:512 * k + UN] for k in range(UH)]
        X, Y, Z = PS[:, 0:1024], PS[:, 1024:2048], PS[:, 2048:3072]
        PB, PC = PS[:, 3072:3072 + P], PS[:, 3584:3584 + P]

        s_w = sem("weights_loaded")
        s_cst = sem("constants_ready")
        s_idx = sem("indices_loaded")
        s_pad = sem("pads_set")
        s_wt = sem("weights_transposed")
        s_x = sem("x_loaded")
        s_tab = {p: sem(f"tables_{p}") for p in PASSES}
        s_g = {p: sem(f"gathered_{p}") for p in PASSES}
        s_old = {p: sem(f"old_{p}") for p in PASSES}
        s_stage, s_bc, s_m, s_cmb, s_new = (sem(n) for n in ("staged", "dst_row", "match", "combined", "new"))
        s_sc = {p: sem(f"scattered_{p}") for p in PASSES}
        s_attr = sem("attr_tile")
        s_held = sem("held")
        s_scrap = sem("scrap")
        s_cn = sem("cnt_loaded")
        s_sq = sem("cnt_plus_one")
        s_sr = sem("cnt_root")
        s_deg = sem("degree_factors")
        s_dv = sem("factors_stored")
        s_rb = sem("factor_row_loaded")
        s_agn = sem("sums_loaded")
        s_ax = sem("sums_transposed")
        s_axf = sem("sums_transposed_free")
        s_at = sem("AT_ready")
        s_xf, s_xfree = sem("X_full"), sem("X_free")
        s_yf, s_yfree = sem("Y_full"), sem("Y_free")
        s_zf, s_zfree = sem("Z_full"), sem("Z_free")
        s_tb = sem("TB_ready")
        s_var = sem("variance")
        s_sd = sem("deviation")
        s_xn = sem("XN_ready")
        s_h = sem("H_ready")
        s_out = sem("stored")
        s_key = sem("keys_ready")
        s_fill = sem("fill_ready")
        s_init = sem("table_cleared")
        s_oh, s_rp, s_rk = sem("key_hot"), sem("rank_counts"), sem("rank_read")
        s_pos, s_pay = sem("positions_staged"), sem("payload_staged")
        s_sct = [sem(f"edges_scattered_{r}") for r in range(SR)]
        s_tabl = [sem("table_loaded_0"), sem("table_loaded_1")]
        s_tt, s_sld = sem("table_turned"), sem("bucket_edges_ready")
        s_ohb, s_bm, s_ev8, s_spm = sem("edge_hot"), sem("block_counted"), sem("block_copied"), sem("block_used")
        s_aw = [[sem(f"block_stored_{b}{a_}") for a_ in range(3)] for b in range(2)]
        s_un = sem("unit_summed")
        s_f1, s_f2, s_flag = sem("flag_parts"), sem("flag_summed"), sem("flag_ready")
        s_at0 = sem("AT_ready_general")
        s_c1, s_c2, s_c3, s_c4 = sem("max_lane"), sem("max_row"), sem("max_one"), sem("max_spread")
        s_hi, s_split = sem("high_ready"), sem("split_ready")
        s_al = [sem(f"adjacency_loaded_{k}") for k in range(RING + 1)]
        s_af = [sem(f"adjacency_free_{k}") for k in range(RING + 1)]
        s_agg = sem("half_summed")
        s_ael = [sem("edge_features_loaded_0"), sem("edge_features_loaded_1")]
        s_aem = sem("edge_features_measured")
        s_nsg = [sem("source_factor_0"), sem("source_factor_1")]
        s_ahl, s_eam, s_eae = sem("edge_split"), sem("edges_summed"), sem("edge_sums_added")
        s_cv = sem("cnt_stored")
        s_d1, s_d2, s_d3, s_d4 = sem("edge_max_lane"), sem("edge_max_row"), sem("edge_max_one"), sem("edge_max_spread")
        s_scale = sem("scale_ready")
        s_res = sem("residual_ready")
        s_row = sem("bias_rows_ready")
        s_aes, s_ahi = sem("edge_features_scaled"), sem("edge_high_ready")

        XU = {0: 0, 1: 7, 4: 14}
        YU = {p: 7 * p for p in range(8)}
        ZU = {4: 0, 5: 7, 6: 14}
        TU = {0: 0, 1: 7, 2: 14, 3: 21, 4: 28, 5: 35, 6: 42}
        LU = {0: 0, 4: 1, 5: 8, 7: 15}
        MEASURED = [0, 2, 3, 4, 5, 7]
        SMALL = [1, 6]
        EDGES = 8
        CU = {p: (k, (s_c1, s_c2, s_c3, s_c4)) for k, p in enumerate([0, 2, 3, 4, 5, 7])}
        CU[EDGES] = (0, (s_d1, s_d2, s_d3, s_d4))
        RES = {4: 1, 5: 2, 7: 3}
        EM = {1: (0, 17), 2: (17, 33), 3: (33, 49)}

        def agu(p):
            return 7 * p + (7 if p >= 4 else 0)

        def atu(p):
            return NU * p

        NGS = [G0[s + 1] - G0[s] for s in range(NU)]

        def scattered(s, r, it=None):
            n = 16 * sum(len(range(r, J, SR)) * NGS[x] for x in range(min(s, NU)))
            return n if it is None else n + (it - r) * (16 // SR) * NGS[s]

        def ahead(u):
            out_ = []
            for b in range(DLO[u], min(DLO[u] + 4, NB)):
                lo, hi = max(P * b, UN * u), min(P * b + P, UN * u + UN)
                if lo < hi:
                    out_.append((b, lo - P * b, lo - UN * u, hi - lo))
            return out_

        def bank(p, k):
            return (Y, Z if p < 2 else Y if p == 4 else X)[k]

        def in_turn(eng, body):
            with eng.Fori(0, NQ // 2) as i:
                for k in range(2):
                    body(2 * i + k, k)
            body(NQ - 1, 0)

        def ring(p):
            r = (TB if p == 5 else HR)[:, :].bitcast(f16)
            return [r[:, k * UH * UN:(k + 1) * UH * UN] for k in range(RING)] + [S5[:, :].bitcast(f16)]

        def iterations(eng, body):
            for r in range(SR):
                body(r, r)
            with eng.Fori(1, J // SR) as i:
                for r in range(SR):
                    body(SR * i + r, r)
            body(J - 1, 0)

        def builds(it):
            return 1 if isinstance(it, int) and it == 16 else 3

        def slots_of(it, a_):
            return 3 if isinstance(it, int) and 3 * it + a_ < 4 else 2

        end = slice((NG - 1) * J, NT)

        block = ctx.enter_context(nc.Block())

        def tiles(eng, body):
            with eng.Fori(0, NG - 1) as g:
                with eng.Fori(0, J) as j:
                    body(g, j, g * J + j, P)
            with eng.Fori(0, J) as j:
                body(NG - 1, j, (NG - 1) * J + j, PTAIL)

        def rows(t):
            return t.rearrange("(b p) f -> p b f", p=P)

        def blk(t):
            return t[:, :].rearrange("p (b f) -> p b f", f=P)

        flags = {}

        def read_flag(eng, name):
            eng.wait_ge(s_flag, 1)
            flags[name] = eng.value_load(flag[0:1, 0:1], min_val=0, max_val=1)

        @block.sync
        def _(sp):
            sp.wait_ge(s_pad, 1)
            for t, name in ((srcI, "src"), (dstI, "dst")):
                v = t[:, :].rearrange("p (g j) -> p g j", j=J)
                sp.dma_start(v[:, 0:NG - 1, :], a[name][0:(NG - 1) * GE].rearrange("(g p j) -> p g j", p=P, j=J)).then_inc(s_idx, 16)
                sp.dma_start(v[0:PTAIL, NG - 1, :], a[name][(NG - 1) * GE:E].rearrange("(p j) -> p j", j=J)).then_inc(s_idx, 16)
            sp.wait_ge(s_fill, 1)
            sp.dma_start(Td.rearrange("(p r) c -> p (r c)", p=P), FILL).then_inc(s_init, 16)
            sp.dma_start(blk(XN)[:, 0:NB - 1, :], rows(a["x"][0:(NB - 1) * P, :])).then_inc(s_x, 16)
            sp.dma_start(blk(XN)[0:NTAIL, NB - 1, :], a["x"][(NB - 1) * P:N, :]).then_inc(s_x, 16)
            for k, w in enumerate(["L0_gnn_W1", "L0_gnn_W2", "L3_gnn_W_l0", "L3_gnn_W_r0", "L3_gnn_W_l1", "L3_gnn_W_r1"]):
                sp.dma_start(WR[:, k, :], a[w][:, :]).then_inc(s_w, 16)
            for k, w in enumerate(["L1_gnn_W1", "L1_gnn_W2", "L1_gnn_W3", "L1_gnn_W4", "L2_gnn_Wn"]):
                sp.dma_start(WN[:, k, :], a[w][:, :]).then_inc(s_w, 16)
            for k in range(2):
                sp.dma_start(We2[DE * k:DE * k + DE, :], a["L2_gnn_We"][:, :]).then_inc(s_w, 16)
            with nc.allow_non_contiguous_dma(reason="a bias of 128 words on partitions"):
                for k, b in enumerate(["L0_gnn_b1", "L1_gnn_b1", "L1_gnn_b2", "L1_gnn_b3"]):
                    sp.dma_start(BC[:, k:k + 1], a[b].rearrange("(p o) -> p o", o=1)).then_inc(s_w, 16)
            for k, b in enumerate(["L0_gnn_b2", "L1_gnn_b4", "L2_gnn_bn", "L2_gnn_be", "L3_gnn_b_l0", "L3_gnn_b_l1"]):
                sp.dma_start(BR[:, k, :], a[b].partition_broadcast(P)).then_inc(s_w, 16)
            sp.dma_start(BR[:, 6, :], a["L2_gnn_resid"][0, :].partition_broadcast(P)).then_inc(s_w, 16)

            for s in range(NU + LAG):
                if 1 <= s <= NU:
                    u = s - 1
                    for r in range(SR):
                        sp.wait_ge(s_sct[r], scattered(s, r))
                    if u >= 2:
                        sp.wait_ge(s_tt, u - 1)
                    t = Td.rearrange("(u n r) c -> u n (r c)", u=NU, n=NB)[u]
                    for n0, sb0, n in ((0, DLO[u], NB - DLO[u]), (NB - DLO[u], 0, DLO[u])):
                        if n:
                            sp.dma_start(TAB[u % 2][n0:n0 + n, :], t[sb0:sb0 + n, :]).then_inc(s_tabl[u % 2], 16)
                u = s - LAG
                if u < 0:
                    continue

                def store(it, r):
                    b = r % 2
                    for a_ in range(builds(it)):
                        n = 3 * it + a_
                        sp.wait_ge(s_ev8, NB * u + n + 1)
                        k = (n + DLO[u]) % NB
                        sp.dma_start(Ad[u // UH][ds(k, 1) if not isinstance(k, int) else slice(k, k + 1), :,
                                                 (u % UH) * UN:(u % UH + 1) * UN].rearrange("o p c -> p (o c)"),
                                     A16[b][a_]).then_inc(s_aw[b][a_], 16)

                iterations(sp, store)
            for b in range(2):
                for a_ in range(3):
                    sp.wait_ge(s_aw[b][a_], 16 * NU * (9 if (b, a_) == (0, 0) else 8))
            read_flag(sp, "sp")

            def tables(p, h, g0):
                sp.dma_start(rows(Hd), h).then_inc(s_tab[p], 16)
                sp.dma_start(rows(Gd), g0).then_inc(s_tab[p], 16)

            flat = [P, NB, P]
            zero = zeros[:, :].unsqueeze(1).to_broadcast(flat)

            def attr_tile(g, j, t, n):
                sp.wait_ge(s_held, t + 1)
                size = GE if n == P else E - (NG - 1) * GE
                sp.dma_start(at[0:n, 0:DE], a["edge_attr_64"][ds(g * GE, size) if n == P else slice(g * GE, E), :]
                             .rearrange("(p j) f -> p j f", j=J)[:, ds(j, 1), :]).then_inc(s_attr, 16)

            def general(p):
                h = blk(XN if p in (0, 6) else HN)
                tables(p, h, h if p in SELF else zero)
                sp.wait_ge(s_sc[p], 16 * NT)
                sp.wait_ge(s_split, 7 * p + 7)
                if p == 4:
                    sp.dma_start(blk(AGN), rows(Ed)).then_inc(s_agn, 16)
                    sp.wait_ge(s_ax, agu(4))
                sp.dma_start(blk(AGN), rows(Gd)).then_inc(s_agn, 16)
                sp.wait_ge(s_agn, 16 * (p + 1 + (p >= 4)))

            with sp.If(flags["sp"]):
                tables("cnt", ones[:, :].unsqueeze(1).to_broadcast(flat), zero)
                sp.wait_ge(s_sc["cnt"], 16 * NT)
                with nc.allow_non_contiguous_dma(reason="one word of each row"):
                    sp.dma_start(CN[:, :], rows(Gd)[:, :, 0]).then_inc(s_cn, 16)
                    sp.wait_ge(s_cn, 16)
                    sp.dma_start(cnt_d.rearrange("(b p) -> p b", p=P), CN[:, :]).then_inc(s_cv, 16)
            with sp.Else():
                sp.wait_ge(s_at, NU)
                sp.dma_start(cnt_d.rearrange("(o n) -> o n", o=1), RB[0:1, :]).then_inc(s_cv, 16)
                sp.sem_inc(s_cn, 16)
            sp.wait_ge(s_cv, 16)
            with nc.allow_non_contiguous_dma(reason="a word of each node"):
                sp.dma_start(CN[:, :], cnt_d.rearrange("(b p) -> p b", p=P)).then_inc(s_cn, 16)
                sp.wait_ge(s_deg, 1)
                sp.dma_start(dinv_d.rearrange("(b p) -> p b", p=P), dinv[:, :]).then_inc(s_dv, 16)
                sp.dma_start(rc_d.rearrange("(b p) -> p b", p=P), rc[:, :]).then_inc(s_dv, 16)
            sp.wait_ge(s_dv, 32)
            sp.dma_start(RB, dinv_d.partition_broadcast(P)).then_inc(s_rb, 16)
            with sp.If(flags["sp"]):
                sp.wait_ge(s_deg, 2)
                tables("attr", blk(HN), zero)
                tiles(sp, attr_tile)
                sp.wait_ge(s_sc["attr"], 16 * NT)
                sp.dma_start(Ed[:, :], Gd[:, :]).then_inc(s_dv, 16)
                sp.wait_ge(s_dv, 48)
                general(0)

            def blocks(p):
                slot = ring(p)
                for h in range(2):
                    n = 2 * (p - 1) + h
                    sp.wait_ge(s_af[RING], n + 1)
                    sp.dma_start(slot[RING], Ad[h][0]).then_inc(s_al[RING], 16)
                    with sp.Fori(0, (NB - 1) // RING) as i:
                        for m in range(RING):
                            sp.wait_ge(s_af[m], 12 * n + i + 1)
                            sp.dma_start(slot[m], Ad[h][ds(RING * i + 1 + m, 1), :, :].rearrange("o p c -> p (o c)")).then_inc(s_al[m], 16)

            for p in range(1, 8):
                if p in (5, 6):
                    sp.wait_ge(s_h, 7 * p)
                if p == 6:
                    sp.dma_start(RB, rc_d.partition_broadcast(P)).then_inc(s_rb, 16)
                with sp.If(flags["sp"]):
                    sp.wait_ge(s_h, 7 * p)
                    general(p)
                with sp.Else():
                    blocks(p)
            for q in range(NQ):
                sp.wait_ge(s_h, 7 * 7 + q + 1)
                b0, b1 = q * QB, (q + 1) * QB - (q == NQ - 1)
                sp.dma_start(rows(out[b0 * P:b1 * P, :]), blk(XN)[:, b0:b1, :]).then_inc(s_out, 16)
            sp.dma_start(out[(NB - 1) * P:N, :], blk(XN)[0:NTAIL, NB - 1, :]).then_inc(s_out, 16)
            sp.wait_ge(s_out, 16 * (NQ + 1))

        @block.gpsimd
        def _(pool):
            g_ = nc.gpsimd
            g_.memset(srcI[:, (NG - 1) * J:], 0)
            g_.memset(dstI[:, (NG - 1) * J:], PADNODE).then_inc(s_pad, 1)
            g_.memset(XN[:, (NB - 1) * P:], 0.0)
            g_.memset(FILL, -1.0).then_inc(s_fill, 1)
            g_.memset(valid[:, :], 0.0)
            g_.memset(at, 0.0)
            g_.memset(zeros[:, :], 0.0)
            g_.memset(ones[:, :], 1.0)
            g_.memset(O16[:, :], 1.0)
            for p in SMALL:
                g_.memset(SC[:, p, 0:1], 2.0 ** (CENTRE - 2))
                g_.memset(SC[:, p, 1:2], 2.0 ** (2 - CENTRE))
            for s in range(NU):
                g_.memset(TG[:, G0[s] * J:G0[s + 1] * J], float(s))
            pool.drain()
            g_.memset(valid[0:PTAIL, :], 1.0)
            g_.iota(gwin[:, :], [[P, NG]], base=-MARGIN, channel_multiplier=0, allow_small_or_imprecise_dtypes=True)
            g_.iota(iot[:, :], [[1, UN]], base=0, channel_multiplier=0, allow_small_or_imprecise_dtypes=True)
            g_.iota(iok[:, :, :], [[64, 2], [1, NB]], base=0, channel_multiplier=0, allow_small_or_imprecise_dtypes=True)
            g_.affine_select(out=Lt[:, :], in_=O16[:, :], compare_op=ALU.is_gt, fill=0.0, base=0, pattern=[[1, P]], channel_multiplier=-1)
            g_.affine_select(out=Uc[:, :], in_=O16[:, :], compare_op=ALU.is_ge, fill=0.0, base=0, pattern=[[-1, P]], channel_multiplier=1)
            g_.affine_select(out=I16[:, :], in_=O16[:, :], compare_op=ALU.is_equal, fill=0.0, base=0, pattern=[[1, P]], channel_multiplier=-1)
            g_.affine_select(out=ident[:, :], in_=ones[:, :], compare_op=ALU.is_equal, fill=0.0, base=0, pattern=[[1, P]], channel_multiplier=-1)
            g_.affine_select(out=low, in_=ones[:, :], compare_op=ALU.is_gt, fill=0.0, base=0,
                             pattern=[[-1, P]], channel_multiplier=1).then_inc(s_cst, 1)

            pool.wait_ge(s_init, 16)
            for s in range(NU):
                def scatter(it, r):
                    n = 17 * s + it + 1
                    pool.wait_ge(s_pay, n)
                    pool.sem_inc(s_scrap, 1)
                    pool.wait_ge(s_pos, n)
                    pool.sem_inc(s_scrap, 1)
                    for a_ in range(NGS[s]):
                        g_.indirect_dma_start(out=Td[:, :], out_offset=bass.IndirectOffsetOnAxis(ap=POS[r][:, a_:a_ + 1], axis=0),
                                              in_=PST[r][:, a_, :], in_offset=None, bounds_check=NU * NB * SLOTS - 1,
                                              oob_is_err=False).then_inc(s_sct[r], 16)

                iterations(pool, scatter)
            pool.wait_ge(s_rk, NT)
            g_.tensor_scalar(TF, SB, float(P), None, ALU.mult)
            g_.tensor_scalar(TG, UU, -float(UN), None, ALU.mult)
            pool.drain()
            g_.tensor_tensor(TF, TF, TG, ALU.add)
            pool.drain()
            g_.tensor_scalar(CAP, TF, -float(P), float(P), ALU.is_gt, ALU.mult)
            g_.tensor_scalar(TG, TF, float(UN), None, ALU.is_lt)
            pool.drain()
            g_.tensor_tensor(CAP, CAP, TG, ALU.mult)
            pool.drain()
            g_.tensor_tensor(RK, RK, CAP, ALU.subtract)
            g_.tensor_tensor(dstF[:, :].rearrange("p (g j) -> p g j", j=J), dstF[:, :].rearrange("p (g j) -> p g j", j=J),
                             gwin[:, :].unsqueeze(2).to_broadcast([P, NG, J]), ALU.subtract)
            pool.drain()
            g_.tensor_scalar(RK, RK, 2.0 * P, None, ALU.is_ge)
            g_.tensor_scalar(TF, dstF[:, :], 0.0, None, ALU.is_lt)
            g_.tensor_scalar(TG, dstF[:, :], float(WIN), None, ALU.is_ge)
            pool.drain()
            g_.tensor_tensor(TF, TF, TG, ALU.add)
            pool.drain()
            g_.tensor_tensor(RK, RK, TF, ALU.add)
            pool.drain()
            g_.tensor_tensor(RK[:, end], RK[:, end], valid[:, :], ALU.mult)
            pool.drain().then_inc(s_f1, 1)
            read_flag(pool, "pool")
            for k in (3, 6):
                g_.tensor_tensor(BR[:, k, :], BR[:, k, :], BR[:, 2, :], ALU.add)
            pool.drain().then_inc(s_row, 1)

            def general(p):
                pool.wait_ge(s_tab[p], 32)

                def tile(g, j, t, n):
                    pool.wait_ge(s_stage, NT * PASSES.index(p) + t + 1)
                    pool.sem_inc(s_scrap, 1)
                    g_.indirect_dma_start(out=msg, out_offset=None, in_=Hd[:, :],
                                          in_offset=bass.IndirectOffsetOnAxis(ap=si[:, 0:1], axis=0)).then_inc(s_g[p], 16)
                    g_.indirect_dma_start(out=old, out_offset=None, in_=Gd[:, :],
                                          in_offset=bass.IndirectOffsetOnAxis(ap=di[:, 0:1], axis=0)).then_inc(s_old[p], 16)
                    pool.wait_ge(s_new, NT * PASSES.index(p) + t + 1)
                    pool.sem_inc(s_scrap, 1)
                    g_.indirect_dma_start(out=Gd[:, :], out_offset=bass.IndirectOffsetOnAxis(ap=xi[:, 0:1], axis=0),
                                          in_=new, in_offset=None, bounds_check=NP - 1,
                                          oob_is_err=False).then_inc(s_sc[p], 16)

                tiles(pool, tile)

            def source_factors():
                table = dinv_d.rearrange("(n o) -> n o", o=1)

                def gather(g, k):
                    g_.tensor_copy(sni[:, k, :], srcI[:, ds(g * J, J)])
                    pool.drain()
                    for j in range(J):
                        g_.indirect_dma_start(out=nsv[:, k, j:j + 1], out_offset=None, in_=table,
                                              in_offset=bass.IndirectOffsetOnAxis(ap=sni[:, k, j:j + 1], axis=0)).then_inc(s_nsg[k], 16)

                def keep(g, k, uses):
                    pool.wait_ge(s_nsg[k], 16 * J * uses)
                    pool.sem_inc(s_scrap, 1)
                    g_.tensor_copy(NS[:, ds(g * J, J)], nsv[:, k, :])

                gather(0, 0)
                with pool.Fori(0, NG // 2) as i:
                    gather(2 * i + 1, 1)
                    keep(2 * i, 0, i + 1)
                    gather(2 * i + 2, 0)
                    keep(2 * i + 1, 1, i + 1)
                keep(NG - 1, 0, NG // 2 + 1)

            def residual_bias(k, n):
                pool.wait_ge(s_h, 7 * n)
                with pool.Fori(0, NQ) as q:
                    x = XN[:, ds(q * QN, QN)].rearrange("p (b f) -> p b f", f=P)
                    g_.tensor_tensor(x, x, BR[:, k, :].unsqueeze(1).to_broadcast([P, QB, P]), ALU.add)
                pool.drain().then_inc(s_res, 1)

            def residual_2():
                pool.wait_ge(s_h, 7 * 5)
                pool.wait_ge(s_zf, ZU[4] + 7)
                with pool.Fori(0, NQ) as q:
                    h = HR[:, ds(q * QN, QN)].rearrange("p (b f) -> p b f", f=P)
                    x = XN[:, ds(q * QN, QN)].rearrange("p (b f) -> p b f", f=P)
                    g_.tensor_tensor(h, h, BR[:, 6, :].unsqueeze(1).to_broadcast([P, QB, P]), ALU.add)
                    pool.drain()
                    g_.tensor_tensor(h, h, idg[:, ds(q * QB, QB)].unsqueeze(2).to_broadcast([P, QB, P]), ALU.mult)
                    pool.drain()
                    g_.tensor_tensor(x, x, h, ALU.add)
                pool.drain().then_inc(s_res, 1)

            def neighbour_rows():
                with pool.Fori(0, NQ) as q:
                    cols = ds(q * QN, QN)
                    pool.wait_ge(s_xfree, q + XU[4] + 2)
                    pool.sem_inc(s_scrap, 1)
                    g_.tensor_tensor(HN[:, cols].rearrange("p (b f) -> p b f", f=P), HR[:, cols].rearrange("p (b f) -> p b f", f=P),
                                     BR[:, 3, :].unsqueeze(1).to_broadcast([P, QB, P]), ALU.add).then_inc(s_row, 1)

            with pool.If(flags["pool"]):
                for p in PASSES:
                    if p == 4:
                        residual_bias(1, 1)
                    if p == 5:
                        neighbour_rows()
                        residual_2()
                    if p == 7:
                        residual_bias(5, 7)
                    general(p)
            with pool.Else():
                pool.wait_ge(s_dv, 32)
                source_factors()
                pool.drain()

                def weighted(g, k, uses):
                    e3 = AE[k].rearrange("p (j f) -> p j f", j=J)
                    pool.wait_ge(s_ael[k], uses)
                    pool.sem_inc(s_scrap, 1)
                    g_.tensor_tensor(e3, e3, NS[:, ds(g * J, J)].unsqueeze(2).to_broadcast([P, J, DE]), ALU.mult).then_inc(s_aes, 1)

                at1 = [16 * ((NG + 1) // 2), 16 * (NG // 2)]
                weighted(0, 0, at1[0] + 16)
                for i0, i1 in ((0, NG // 4), (NG // 4, NG // 2)):
                    if i0:
                        residual_bias(1, 1)
                    with pool.Fori(i0, i1) as i:
                        weighted(2 * i + 1, 1, at1[1] + 16 + 16 * i)
                        weighted(2 * i + 2, 0, at1[0] + 32 + 16 * i)
                neighbour_rows()
                residual_2()
                residual_bias(5, 7)

        @block.vector
        def _(dve):
            v = nc.vector

            def three(ap):
                return ap.rearrange("p (b f) -> p b f", f=P)

            dve.wait_ge(s_idx, 64)
            dve.wait_ge(s_cst, 1)
            v.tensor_scalar(TI, srcI[:, :], 7, None, ALU.logical_shift_right)
            v.tensor_copy(dstF[:, :], dstI[:, :])
            dve.drain()
            v.tensor_copy(SB, TI)
            dve.drain()
            v.tensor_scalar(TI, srcI[:, :], P - 1, None, ALU.bitwise_and)
            dve.drain()
            v.tensor_copy(PAY[:, :, 0], TI)
            dve.drain()
            v.tensor_scalar(TI, dstI[:, :], 6, None, ALU.logical_shift_right)
            dve.drain()
            v.tensor_scalar(TF, TI, 1.0 / 7.0, 0.5 / 7.0 - 0.5, ALU.mult, ALU.add)
            dve.drain()
            v.tensor_scalar(UU, TF, 12582912.0, -12582912.0, ALU.add, ALU.add)
            dve.drain()
            v.scalar_tensor_tensor(out=PAY[:, :, 1], in0=UU, scalar=-float(UN), in1=dstF[:, :], op0=ALU.mult, op1=ALU.add)
            v.scalar_tensor_tensor(out=BASE, in0=UU, scalar=float(NB), in1=SB, op0=ALU.mult, op1=ALU.add)
            v.tensor_tensor(TF, UU, TG, ALU.subtract)
            dve.drain()
            v.tensor_scalar(BASE, BASE, float(SLOTS), None, ALU.mult)
            v.scalar_tensor_tensor(out=KEY, in0=TF, scalar=64.0, in1=SB, op0=ALU.mult, op1=ALU.add)
            dve.drain()
            v.scalar_tensor_tensor(out=KEY[:, end], in0=KEY[:, end], scalar=1.0, in1=valid[:, :], op0=ALU.add, op1=ALU.mult)
            v.scalar_tensor_tensor(out=BASE[:, end], in0=BASE[:, end], scalar=-FAR, in1=valid[:, :], op0=ALU.add, op1=ALU.mult)
            dve.drain()
            v.tensor_scalar(KEY[:, end], KEY[:, end], -1.0, None, ALU.add)
            v.tensor_scalar(BASE[:, end], BASE[:, end], FAR, None, ALU.add).then_inc(s_key, 1)
            dve.drain()
            v.tensor_copy(KEY16, KEY)
            dve.drain()

            def measure(p):
                n, (lane, line, one, spread) = CU[p]
                v.tensor_reduce(mx[:, :], MX[:, :], axis=AX, op=ALU.max).then_inc(lane, 1)
                dve.wait_ge(line, n + 1)
                v.tensor_reduce(m1[:, :], CH[0:1, 0:P], axis=AX, op=ALU.max).then_inc(one, 1)
                dve.wait_ge(spread, n + 1)
                v.tensor_scalar(mc[:, :], CH[:, P:P + 1], 1e-30, None, ALU.max)
                dve.drain()
                v.tensor_scalar(me[:, :], mc[:, :].bitcast(i32), 0x7F800000, None, ALU.bitwise_and)
                dve.drain()
                v.tensor_scalar(SC[:, p, 0:1].bitcast(i32), me[:, :], -1.0, float((254 + CENTRE) << 23), ALU.mult, ALU.add)
                v.tensor_scalar(SC[:, p, 1:2].bitcast(i32), me[:, :], float(-(CENTRE << 23)), None, ALU.add)
                dve.drain()

            def low_half(p, q, source):
                cols = ds(q * QN, QN)
                dve.wait_ge(s_hi, q + 7 * p + 1)
                v.scalar_tensor_tensor(out=LO[:, cols], in0=source[:, cols], scalar=SC[:, p, 0:1], in1=HI[:, cols],
                                       op0=ALU.mult, op1=ALU.subtract).then_inc(s_split, 1)

            def split(p, source):
                dve.drain().then_inc(s_scale, 1)
                with dve.Fori(0, NQ) as q:
                    low_half(p, q, source)

            def prelude():
                dve.wait_ge(s_wt, 1)
                v.tensor_copy(WT[:, :, :].rearrange("p k f -> p (k f)"), WTP)
                dve.wait_ge(s_x, 32)
                for q in range(NQ):
                    v.tensor_reduce(MX[:, q:q + 1], XN[:, q * QN:(q + 1) * QN], axis=AX, op=ALU.max, apply_absolute_value=True)
                dve.drain()
                measure(0)
                split(0, XN)

            for s in range(NU + LAG):
                u = s - LAG
                if s == 1:
                    prelude()
                def indicators(m, k_, part=None):
                    n = NB * u + m
                    ks = range(3 if isinstance(m, int) and m < 4 else 2)
                    if part is not None:
                        ks = ks[:1] if part == 0 else ks[1:]
                    if part == 1:
                        pass
                    elif isinstance(m, int) and m == 0:
                        if n:
                            dve.wait_ge(s_bm, n)
                    elif not (isinstance(n, int) and n <= 2):
                        dve.wait_ge(s_bm, n - 2)
                    if part != 1:
                        n_ = 3 if isinstance(m, int) and m < 4 else 2
                        v.tensor_tensor(OHS[k_][:, 0:n_, :], iot[:, 0:P].unsqueeze(1).to_broadcast([P, n_, P]),
                                        S16[u % 2][:, 0:n_, ds(m, 1)].to_broadcast([P, n_, P]), ALU.is_equal)
                    for k in ks:
                        last = v.tensor_scalar(OHD[k_][k], iot[:, :], SLD[u % 2][:, 2 * k + 1, ds(m, 1)], None, ALU.is_equal)
                    if part != 0:
                        last.then_inc(s_ohb, 1)

                def hot(it, r, ng):
                    v.tensor_tensor(OHK[(r + s) % 2][:, 0:ng, :], iok[:, :, :].rearrange("p a c -> p (a c)").unsqueeze(1).to_broadcast([P, ng, 2 * NB]),
                                    KEY16.rearrange("p (g j) -> p g j", j=J)[:, G0[s]:G0[s] + ng, ds(it, 1)].to_broadcast([P, ng, 2 * NB]),
                                    ALU.is_equal).then_inc(s_oh, 1)

                def positions(it, r, ng):
                    dve.wait_ge(s_rk, G0[s] * J + (it + 1) * ng)
                    if s or not isinstance(it, int) or it >= SR:
                        dve.wait_ge(s_sct[r], scattered(s, r, it))
                        dve.sem_inc(s_scrap, 1)
                    cols = slice(G0[s], G0[s] + ng)
                    v.tensor_tensor(POS[r][:, 0:ng].unsqueeze(2),
                                    RK.rearrange("p (g j) -> p g j", j=J)[:, cols, ds(it, 1)],
                                    BASE.rearrange("p (g j) -> p g j", j=J)[:, cols, ds(it, 1)], ALU.add).then_inc(s_pos, 1)

                def step(it, r):
                    b = r % 2
                    ng = NGS[s] if s < NU else 0
                    nb = builds(it) if u >= 0 else 0
                    n0 = G0[min(s, NU)] * J + it * ng

                    for a_ in range(max(ng, nb)):
                        if nb == 3:
                            for m, part in ([[(1, None)], [(2, 0)], [(2, 1), (3, 0)], [(3, 1)]] if ng == 4 else
                                            [[(1, None)], [(2, None)], [(3, None)]])[a_]:
                                indicators(3 * it + m, m % 3, part)
                        if ng and a_ == ng - 1 and not (isinstance(it, int) and it == J - 1):
                            hot(it + 1, r + 1, ng)
                        if a_ == 0 and ng and not (isinstance(it, int) and it < 2):
                            positions(it - 1, (r - 1) % SR, ng)
                        if a_ < ng:
                            dve.wait_ge(s_rp, n0 + a_ + 1)
                            t = ds((G0[s] + a_) * J + it, 1)
                            v.scalar_tensor_tensor(out=JK[a_].rearrange("p (a c) -> p a c", a=2), in0=iok[:, :, :], scalar=KEY[:, t],
                                                   in1=RP[:, 64 * s:64 * s + 128].rearrange("p (a c) -> p a c", a=2)[:, :, 0:NB],
                                                   op0=ALU.is_equal, op1=ALU.mult, accum_out=RK[:, t]).then_inc(s_rk, 1)
                    if ng and isinstance(it, int) and it in (0, J - 1):
                        positions(it, r, ng)

                if u >= 0:
                    dve.wait_ge(s_sld, u + 1)
                    indicators(0, 0)
                if s < NU:
                    hot(0, 0, NGS[s])
                iterations(dve, step)

            dve.wait_ge(s_f1, 1)
            v.tensor_reduce(fl[:, 0:1], RK, axis=AX, op=ALU.max).then_inc(s_f1, 1)
            dve.wait_ge(s_f2, 1)
            v.tensor_scalar(flag[:, :], CH[:, 0:1], 0.5, None, ALU.is_gt).then_inc(s_flag, 1)
            read_flag(dve, "dve")

            def general(p):
                def tile(g, j, t, n):
                    m = NT * PASSES.index(p) + t + 1
                    v.tensor_copy(si[:, :], srcI[:, ds(t, 1)])
                    v.tensor_copy(di[:, :], dstI[:, ds(t, 1)])
                    v.tensor_scalar(Dg, ident[:, :], dstF[:, ds(t, 1)], None, ALU.mult).then_inc(s_stage, 1)
                    dve.wait_ge(s_bc, m)
                    v.tensor_scalar(M, PB, dstF[:, ds(t, 1)], None, ALU.is_equal)
                    dve.drain()
                    v.tensor_tensor_reduce(out=ML, in0=M, in1=low, scale=1.0, scalar=0.0,
                                           op0=ALU.mult, op1=ALU.add, accum_out=cl[:, :])
                    dve.drain()
                    v.tensor_scalar(far[:, :], cl[:, :], 0.5, FAR, ALU.is_gt, ALU.mult)
                    dve.drain()
                    dve.wait_ge(s_g[p], 16 * (t + 1))
                    if p == "attr":
                        v.tensor_tensor(xi[:, :], far[:, :], dstF[:, ds(t, 1)], ALU.add)
                        dve.wait_ge(s_attr, 16 * (t + 1))
                        v.tensor_tensor(msg, msg, at, ALU.mult).then_inc(s_m, 1)
                        dve.drain().then_inc(s_held, 1)
                    else:
                        v.tensor_tensor(xi[:, :], far[:, :], dstF[:, ds(t, 1)], ALU.add).then_inc(s_m, 1)
                    dve.wait_ge(s_cmb, m)
                    dve.sem_inc(s_scrap, 1)
                    dve.wait_ge(s_old[p], 16 * (t + 1))
                    v.tensor_tensor(new, PC, old, ALU.add).then_inc(s_new, 1)
                    dve.wait_ge(s_sc[p], 16 * (t + 1))
                    dve.sem_inc(s_scrap, 1)

                tiles(dve, tile)

            def general_sums(p, done, n):
                with dve.Fori(0, NQ) as q:
                    dve.wait_ge(s_ax, agu(p) + q + 1)
                    cols = ds(q * QN, QN)
                    if p in (1, 2, 3, 6, 7):
                        v.tensor_tensor(AT[:, cols], X[:, 0:QN], RB[:, cols], ALU.mult).then_inc(done, n)
                    else:
                        v.tensor_copy(AT[:, cols], X[:, 0:QN]).then_inc(done, n)
                    dve.drain().then_inc(s_axf, 1)

            with dve.If(flags["dve"]):
                v.tensor_copy(dstF[:, :], dstI[:, :])
                dve.drain()
                general("cnt")
            dve.wait_ge(s_cn, 32)
            v.tensor_scalar(c1[:, :], CN[:, :], 1.0, None, ALU.add).then_inc(s_sq, 1)
            v.tensor_scalar(c2[:, :], CN[:, :], 1.0, None, ALU.max)
            dve.wait_ge(s_sr, 1)
            v.reciprocal(dinv[:, :], SQ[:, :])
            dve.drain()
            v.reciprocal(idg[:, :], c1[:, :])
            v.reciprocal(rc[:, :], c2[:, :]).then_inc(s_deg, 1)
            dve.drain()
            with dve.If(flags["dve"]):
                v.tensor_copy(blk(HN), dinv[:, :].unsqueeze(2).to_broadcast([P, NB, P])).then_inc(s_deg, 1)
                dve.sem_inc(s_held, 1)
                general("attr")
                general(0)
                general_sums(0, s_at0, 1)

            def row(k):
                return BR[:, k, :].unsqueeze(1).to_broadcast([P, QB, P])

            def of(t, q):
                return t[:, ds(q * QB, QB)].unsqueeze(2).to_broadcast([P, QB, P])

            def statistics(q, at_=None):
                dve.drain()
                for b in range(QB):
                    st = ST[:, b, :] if at_ == 0 else ST[:, ds(q * QB + b, 1), :].rearrange("p o c -> p (o c)")
                    v.bn_stats(st, HN[:, ds(q * QN + b * P, P)])

            def deviations(blocks, n):
                dve.drain()
                for b in range(blocks):
                    v.bn_aggr(MV[:, b, :], ST[:, b, :])
                dve.drain()
                v.tensor_scalar(VE[:, 0:blocks], MV[:, 0:blocks, 1], EPS, None, ALU.add).then_inc(s_var, 1)
                dve.wait_ge(s_sd, n)
                v.reciprocal(RS[:, 0:blocks], SD[:, 0:blocks])
                dve.drain()

            def normalise(q, at_=None):
                for b in range(QB):
                    cols = ds(q * QN + b * P, P)
                    m, r = (MV[:, b, 0:1], RS[:, b:b + 1]) if at_ == 0 else (MV[:, ds(q * QB + b, 1), 0], RS[:, ds(q * QB + b, 1)])
                    last = v.tensor_scalar(XN[:, cols], HN[:, cols], m, r, ALU.subtract, ALU.mult)
                return last

            def biggest(q):
                v.tensor_reduce(MX[:, ds(q, 1)], HN[:, ds(q * QN, QN)], axis=AX, op=ALU.max, apply_absolute_value=True)

            def after(p):
                def leave(q, k):
                    cols = ds(q * QN, QN)
                    h, x, y = HN[:, cols], XN[:, cols], bank(p, k)[:, 0:QN]
                    dve.wait_ge(s_yf, q + YU[p] + 1)
                    if p in (0, 6):
                        v.tensor_tensor(three(h), three(y), row(0 if p == 0 else 4), ALU.add).then_inc(s_yfree, 1)
                        dve.drain()
                    if p == 0:
                        v.scalar_tensor_tensor(out=h, in0=h, scalar=0.0, in1=x, op0=ALU.max, op1=ALU.add)
                    elif p in (1, 2, 3, 4, 5):
                        v.tensor_tensor(three(h), three(y), of(dinv, q), ALU.mult).then_inc(s_yfree, 1)
                    elif p == 6:
                        v.tensor_scalar(h, h, 0.0, None, ALU.max)
                    else:
                        v.tensor_tensor(h, y, x, ALU.add).then_inc(s_yfree, 1)
                    if p in (4, 5):
                        dve.drain()
                        v.tensor_tensor(h, h, x, ALU.add)
                    if p in (1, 2, 3, 6):
                        dve.drain().then_inc(s_h, 1)
                        biggest(q)
                    elif p == 0:
                        statistics(q)
                    else:
                        statistics(q, 0)
                        deviations(QB, q + LU[p] + 1)
                        normalise(q, 0).then_inc(s_h if p == 7 else s_xn, 1)
                        if p == 5:
                            dve.drain().then_inc(s_h, 1)

                if p in RES:
                    dve.wait_ge(s_res, RES[p])
                in_turn(dve, leave)

                if p == 0:
                    deviations(NB, LU[p] + 1)

                    def finish(q):
                        cols = ds(q * QN, QN)
                        normalise(q)
                        dve.drain()
                        v.tensor_tensor(three(HN[:, cols]), three(XN[:, cols]), of(dinv, q), ALU.mult).then_inc(s_h, 1)

                    finish(0)
                    with dve.Fori(1, NQ) as q:
                        finish(q)
                        low_half(1, q - 1, HN)
                    low_half(1, NQ - 1, HN)
                    return
                if p == 5:
                    with dve.Fori(0, NQ) as q:
                        low_half(6, q, XN)
                    return
                if p == 4:
                    with dve.Fori(0, NQ) as q:
                        cols = ds(q * QN, QN)
                        dve.wait_ge(s_row, q + 2)
                        v.tensor_tensor(three(HN[:, cols]), three(HN[:, cols]), of(dinv, q), ALU.mult)
                        dve.drain().then_inc(s_h, 1)
                        biggest(q)
                if p < 7:
                    dve.drain()
                    measure(p + 1)
                    split(p + 1, HN)

            def fast_sums(p, h):
                dve.wait_ge(s_agg, 2 * (p - 1) + h + 1)
                for k in range(UH):
                    cols = slice((UH * h + k) * UN, (UH * h + k + 1) * UN)
                    if p in (1, 2, 3, 6, 7):
                        v.scalar_tensor_tensor(out=AT[:, cols], in0=AGB[k], scalar=SC[:, p, 1:2], in1=RB[:, cols],
                                               op0=ALU.mult, op1=ALU.mult).then_inc(s_at, 1)
                    else:
                        v.tensor_scalar(AT[:, cols], AGB[k], SC[:, p, 1:2], None, ALU.mult).then_inc(s_at, 1)

            def edge_measure(g0, g1):
                def group(g, k, uses):
                    dve.wait_ge(s_ael[k], 16 * uses)
                    v.tensor_reduce(MXE[:, ds(g, 1)], AE[k], axis=AX, op=ALU.max, apply_absolute_value=True).then_inc(s_aem, 1)

                pairs = (g1 - g0) // 2
                with dve.Fori(0, pairs) as i:
                    for m in range(2):
                        group(2 * i + g0 + m, (g0 + m) % 2, i + (g0 + m) // 2 + 1)
                for g in range(g0 + 2 * pairs, g1):
                    group(g, g % 2, g // 2 + 1)

            def edge_sums():
                v.tensor_reduce(MX[:, :], MXE[:, :].rearrange("p (q g) -> p q g", q=NQ), axis=AX, op=ALU.max)
                dve.drain()
                measure(EDGES)
                dve.drain().then_inc(s_aem, 1)
                v.memset(RBW[:, :], 0.0)
                dve.drain()

                def add(g):
                    dve.wait_ge(s_eam, g + 2)
                    win = RBW[:, ds(P * g, WIN)]
                    v.scalar_tensor_tensor(out=win, in0=CH[:, 0:WIN], scalar=SC[:, EDGES, 1:2], in1=win,
                                           op0=ALU.mult, op1=ALU.add).then_inc(s_eae, 1)

                def group(g, k):
                    e3 = AE[k].rearrange("p (j f) -> p j f", j=J)
                    if not isinstance(g, int):
                        dve.wait_ge(s_eam, g)
                    for j in range(J):
                        v.tensor_scalar(OHW[k][:, j, :], iot[:, 0:WIN], dstF[:, ds(g * J + j, 1)], None, ALU.is_equal)
                    dve.wait_ge(s_ahi, g + 1)
                    v.scalar_tensor_tensor(out=AHL[k][:, :, DE:2 * DE], in0=e3, scalar=SC[:, EDGES, 0:1], in1=AHL[k][:, :, 0:DE],
                                           op0=ALU.mult, op1=ALU.subtract).then_inc(s_ahl, 1)

                def pairs(i0, i1):
                    with dve.Fori(i0, i1) as i:
                        for m in range(2):
                            g = 2 * i + 1 + m
                            k = (m + 1) % 2
                            group(g, k)
                            dve.drain()
                            add(g - 1)
                            dve.drain()

                group(0, 0)
                pairs(0, 6)
                fast_sums(4, 0)
                pairs(6, (NG - 1) // 2)
                add(NG - 1)
                dve.drain()
                fast_sums(4, 1)

            after(0)
            for p in range(1, 8):
                if p in (1, 6):
                    dve.wait_ge(s_rb, 16 if p == 1 else 32)
                with dve.If(flags["dve"]):
                    general(p)
                    general_sums(p, s_at, 2)
                with dve.Else():
                    if p in EM:
                        edge_measure(*EM[p])
                    if p == 4:
                        edge_sums()
                    else:
                        fast_sums(p, 0)
                        fast_sums(p, 1)
                after(p)

        @block.scalar
        def _(act):
            c = nc.scalar

            def high(p, q, source):
                cols = ds(q * QN, QN)
                c.activation(HI[:, cols], source[:, cols], ACT.Copy, scale=SC[:, p, 0:1]).then_inc(s_hi, 1)

            def highs_of(p, source, count):
                act.wait_ge(s_scale, count)
                with act.Fori(0, NQ) as q:
                    high(p, q, source)

            act.wait_ge(s_key, 1)
            for s in range(NU + LAG):
                u = s - LAG
                if s == 1:
                    highs_of(0, XN, 1)

                def step(it, r):
                    b = r % 2
                    if 1 <= s <= NU and isinstance(it, int) and it == J - 1:
                        w = s - 1
                        if w >= 2:
                            act.wait_ge(s_ohb, NB * (w - 1))
                        act.wait_ge(s_tt, w + 1)
                        c.copy(S16[w % 2], TP[:, 0:6 * 64].rearrange("p (k c n) -> p k c n", k=3, c=2)[:, :, 0, 0:NB])
                        c.copy(SLD[w % 2], TP[:, 0:6 * 64].rearrange("p (k n) -> p k n", n=64)[:, :, 0:NB]).then_inc(s_sld, 1)
                    if s < NU:
                        if s or not isinstance(it, int) or it >= SR:
                            act.wait_ge(s_sct[r], scattered(s, r, it))
                            act.sem_inc(s_scrap, 1)
                        ng = NGS[s]
                        c.copy(PST[r][:, 0:ng, :],
                               PAY.rearrange("p (g j) c -> p g j c", j=J)[:, G0[s]:G0[s] + ng, ds(it, 1), :].rearrange("p g o c -> p g (o c)")
                               ).then_inc(s_pay, 1)
                    if u < 0:
                        return
                    for a_ in range(builds(it)):
                        n = NB * u + 3 * it + a_
                        if isinstance(it, int) and 3 * it + a_ == 0:
                            if n:
                                act.wait_ge(s_spm, n)
                        elif not isinstance(n, int) or n > 5:
                            act.wait_ge(s_spm, n - 5)
                            act.sem_inc(s_scrap, 1)
                        use = u * (9 if (b, a_) == (0, 0) else 8)
                        if isinstance(it, int):
                            if use + it // 2:
                                act.wait_ge(s_aw[b][a_], 16 * (use + it // 2))
                        else:
                            act.wait_ge(s_aw[b][a_], 8 * (it - b) + 16 * use)
                            act.sem_inc(s_scrap, 1)
                        act.wait_ge(s_bm, n + 1)
                        c.copy(A16[b][a_], BP[a_]).then_inc(s_ev8, 1)

                iterations(act, step)
                if u >= 0:
                    cols = slice(UN * u, UN * (u + 1))
                    act.wait_ge(s_un, u + 1)
                    c.copy(RB[:, cols], CNT)
                    c.activation(AT[:, cols], AGG, ACT.Copy, scale=SC[:, 0, 1:2]).then_inc(s_at, 1)
            read_flag(act, "act")
            act.wait_ge(s_sq, 1)
            c.activation(SQ[:, :], c1[:, :], ACT.Sqrt).then_inc(s_sr, 1)

            def root(n, blocks):
                act.wait_ge(s_var, n)
                c.activation(SD[:, 0:blocks], VE[:, 0:blocks], ACT.Sqrt).then_inc(s_sd, 1)

            def load(g, k, full=True):
                n = P if full else PTAIL
                act.dma_start(AE[k][0:n, :], a["edge_attr_64"][ds(g * GE, GE) if full else slice(g * GE, E), :]
                              .rearrange("(p j) f -> p (j f)", j=J)).then_inc(s_ael[k], 16)

            def reload(g, k, full=True):
                act.wait_ge(s_aem, g - 1)
                load(g, k, full)

            for p in range(8):
                if p == 4:
                    with act.If(flags["act"]):
                        with act.Fori(0, NQ) as q:
                            act.wait_ge(s_ax, agu(4) - 7 + q + 1)
                            c.copy(RB[:, ds(q * QN, QN)], X[:, 0:QN])
                            act.drain().then_inc(s_axf, 1)
                    with act.Else():
                        act.wait_ge(s_yf, YU[3] + 7)
                        load(0, 0)
                        load(1, 1)
                        act.wait_ge(s_split, 7 * 4 + 7)
                        act.wait_ge(s_aem, NG + 1)

                        def highs(g, k):
                            if not (isinstance(g, int) and g == 0):
                                act.wait_ge(s_eam, g)
                                act.sem_inc(s_scrap, 1)
                            act.wait_ge(s_aes, g + 1)
                            c.activation(AHL[k][:, :, 0:DE], AE[k].rearrange("p (j f) -> p j f", j=J), ACT.Copy,
                                         scale=SC[:, EDGES, 0:1]).then_inc(s_ahi, 1)

                        def refill(g, k, full=True):
                            act.wait_ge(s_ahl, g - 1)
                            load(g, k, full)

                        highs(0, 0)
                        refill(2, 0)
                        with act.Fori(0, (NG - 1) // 4 - 1) as i:
                            for m in range(4):
                                highs(4 * i + 1 + m, (m + 1) % 2)
                                refill(4 * i + 3 + m, (m + 1) % 2)
                        for g in range(NG - 4, NG):
                            highs(g, g % 2)
                            if g + 2 < NG:
                                refill(g + 2, g % 2, g + 2 < NG - 1)
                if p in EM:
                    g0, g1 = EM[p]
                    with act.If(flags["act"]):
                        act.sem_inc(s_scrap, 1)
                    with act.Else():
                        act.wait_ge(s_yf, YU[p - 1] + 7)
                        for g in (g0, g0 + 1):
                            if g < 2:
                                load(g, g % 2)
                            else:
                                reload(g, g % 2)
                        pairs = (g1 - g0) // 2
                        with act.Fori(1, pairs - 1) as i:
                            for m in range(2):
                                reload(2 * i + g0 + m, (g0 + m) % 2)
                        for g in range(g0 + 2 * (pairs - 1), g1):
                            reload(g, g % 2, g < NG - 1)
                if p in (0, 1):
                    with act.Fori(0, NQ) as q:
                        act.wait_ge(s_xf, XU[p] + q + 1)
                        for h in range(2):
                            c.activation(TB[:, ds(q * QN + h * UN, UN)], X[:, 512 * h:512 * h + UN], ACT.Relu, bias=BC[:, p:p + 1])
                        act.drain().then_inc(s_tb, 1)
                        act.sem_inc(s_xfree, 1)
                    if p == 0:
                        root(LU[p] + 1, NB)
                        with act.Fori(0, NQ) as q:
                            act.wait_ge(s_h, q + 1)
                            high(1, q, HN)
                elif p in (2, 3):
                    with act.Fori(0, NQ) as q:
                        act.wait_ge(s_at, atu(p) + 2 * q + 2)
                        cols = ds(q * QN, QN)
                        c.activation(TB[:, cols], AT[:, cols], ACT.Relu, bias=BC[:, p:p + 1]).then_inc(s_tb, 1)
                elif p in (4, 5, 6):
                    def turned(q):
                        act.wait_ge(s_zf, q + ZU[p] + 1)
                        c.copy(TB[:, ds(q * QN, QN)], Z[:, 0:QN])
                        act.drain().then_inc(s_tb, 1)
                        act.sem_inc(s_zfree, 1)
                        if p == 5:
                            high(6, q, XN)

                    def keep(q):
                        act.wait_ge(s_xf, q + XU[4] + 1)
                        c.copy(HR[:, ds(q * QN, QN)], X[:, 0:QN]).then_inc(s_xfree, 1)

                    if p == 4:
                        for q in range(2):
                            root(LU[p] + q + 1, QB)
                        root(LU[p] + 3, QB)
                        turned(0)
                        with act.Fori(3, NQ) as q:
                            root(q + LU[p] + 1, QB)
                            turned(q - 2)
                            keep(q - 3)
                        turned(NQ - 2)
                        keep(NQ - 3)
                        turned(NQ - 1)
                        keep(NQ - 2)
                        keep(NQ - 1)
                    elif p == 5:
                        root(LU[p] + 1, QB)
                        root(LU[p] + 2, QB)
                        with act.Fori(2, NQ) as q:
                            root(q + LU[p] + 1, QB)
                            turned(q - 2)
                        turned(NQ - 2)
                        turned(NQ - 1)
                    else:
                        with act.Fori(0, NQ) as q:
                            turned(q)
                else:
                    with act.Fori(0, NQ) as q:
                        root(q + LU[p] + 1, QB)
                if p < 7 and p not in (0, 5):
                    highs_of(p + 1, HN, 1 + len([x for x in MEASURED if 0 < x <= p + 1]))

        @block.tensor
        def _(pe):
            t_ = nc.tensor

            def mm(out_, w, m, start=False):
                return t_.matmul(out_, w, m, start=start, stop=True, skip_group_check=True)

            pe.wait_ge(s_cst, 1)
            z16 = zeros[:, :].bitcast(f16)[:, 0:P]
            for k in range(2):
                mm(PS[:, 512 * k:512 * k + UN], z16, iot[:, :], start=True)
                mm(PS[:, 512 * k + UN:512 * k + 512], z16, iot[:, 0:512 - UN])
            for e in [s_xfree, s_yfree, s_zfree, s_axf, s_eam, s_eae] + s_af:
                pe.sem_inc(e, 1)

            def measured(p):
                n, (lane, line, one, spread) = CU[p]
                pe.wait_ge(lane, n + 1)
                t_.matmul(CH[0:1, 0:P], mx[:, 0:1], ident[:, :], start=True, stop=True).then_inc(line, 1)
                pe.wait_ge(one, n + 1)
                t_.matmul(CH[:, P:P + 1], ones[0:1, :], m1[0:1, 0:1], start=True, stop=True).then_inc(spread, 1)

            for s in range(NU + LAG):
                u = s - LAG
                if s == 1:
                    pe.wait_ge(s_w, 16 * 24)
                    for k in range(6):
                        last = t_.transpose(WTP[:, k * P:(k + 1) * P], WR[:, k, :], ident[:, :])
                    last.then_inc(s_wt, 1)
                    measured(0)
                if u == 0:
                    pe.wait_ge(s_split, NQ)

                def used(n, b, a_, first):
                    k = (n + DLO[u]) % NB
                    cols = ds(k * P, P) if not isinstance(k, int) else slice(k * P, k * P + P)
                    mm(AGG, HI[:, cols], A16[b][a_], start=first)
                    mm(AGG, LO[:, cols], A16[b][a_])
                    mm(CNT, O16[:, :], A16[b][a_], start=first).then_inc(s_spm, 1)

                def step(it, r):
                    b = r % 2
                    ng = NGS[s] if s < NU else 0
                    nb = builds(it) if u >= 0 else 0
                    if 1 <= s <= NU and isinstance(it, int) and it == J - 1:
                        w = s - 1
                        pe.wait_ge(s_tabl[w % 2], 16 * sum(2 if DLO[x] else 1 for x in range(w % 2, w + 1, 2)))
                        if w:
                            pe.wait_ge(s_sld, w)
                        tab = TAB[w % 2].rearrange("p (r c) -> p r c", c=2)
                        for k in range(3):
                            for c in range(2):
                                q = 64 * (2 * k + c)
                                last = t_.transpose(TP[:, q:q + NB], tab[0:NB, P * k:P * (k + 1), c], I16[0:NB, 0:NB])
                        last.then_inc(s_tt, 1)
                    both = range(2 if s + 1 < NU else 1)
                    t0 = G0[min(s, NU)] * J + it * ng

                    def count(w, a_):
                        for k in both:
                            last = mm(RP[:, 64 * (s + k):64 * (s + k) + NB], w[:, :], OHK[(r + s) % 2][:, a_, NB * k:NB * k + NB])
                        return last

                    def rank(a_):
                        if a_ == 0:
                            pe.wait_ge(s_oh, J * s + it + 1)
                        count(Lt, a_).then_inc(s_rp, 1)

                    if ng:
                        rank(0)
                    for a_ in range(max(ng, nb)):
                        n = 3 * it + a_
                        N_ = NB * u + n
                        first = isinstance(n, int) and n == 0
                        if a_ < nb:
                            pe.wait_ge(s_ohb, N_ + 1)
                            if not (isinstance(N_, int) and N_ < 3):
                                pe.wait_ge(s_ev8, N_ if first else N_ - 2)
                            for k in range(slots_of(it, a_)):
                                last = mm(BP[a_], OHS[a_][:, k, :], OHD[a_][k], start=k == 0)
                            last.then_inc(s_bm, 1)
                        if a_ < ng:
                            pe.wait_ge(s_rk, t0 + a_ + 1)
                            count(Uc, a_)
                            if a_ + 1 < ng:
                                rank(a_ + 1)
                        if a_ < nb and not first:
                            if isinstance(n, int) and n == 1 and u:
                                pe.wait_ge(s_at, u)
                            pe.wait_ge(s_ev8, N_)
                            used(n - 1, b if a_ else 1 - b, (a_ - 1) % 3, isinstance(n, int) and n == 1)

                iterations(pe, step)
                if u >= 0:
                    pe.wait_ge(s_ev8, NB * (u + 1))
                    used(NB - 1, 0, 0, False)
                    for blk_, c0, d0, w_ in ahead(u):
                        for part in (HI, LO):
                            mm(AGG[:, d0:d0 + w_], part[:, blk_ * P:(blk_ + 1) * P], I16[:, c0:c0 + w_])
                    pe.drain().then_inc(s_un, 1)
            pe.wait_ge(s_f1, 2)
            t_.matmul(CH[:, 0:1], ones[:, :], fl[:, 0:1], start=True, stop=True).then_inc(s_f2, 1)
            read_flag(pe, "pe")

            def general(p):
                def tile(g, j, t, n):
                    m = NT * PASSES.index(p) + t + 1
                    pe.wait_ge(s_stage, m)
                    t_.matmul(PB, ones[:, :], Dg, start=True, stop=True).then_inc(s_bc, 1)
                    pe.wait_ge(s_m, m)
                    t_.matmul(PC, M, msg, start=True, stop=True).then_inc(s_cmb, 1)

                tiles(pe, tile)

            def sums(n, loaded):
                pe.wait_ge(s_agn, 16 * loaded)
                for q in range(NQ):
                    pe.wait_ge(s_axf, n + q + 1)
                    for b in range(QB):
                        last = t_.transpose(X[:, b * P:(b + 1) * P], AGN[:, ds(q * QN + b * P, P)], ident[:, :])
                    last.then_inc(s_ax, 1)

            def node_stage(p, n, q, parts):
                y = bank(p, q % 2)
                pe.wait_ge(s_yfree, n + q + (1 if q == 0 or p == 4 else 0))
                if q < 2 and p:
                    pe.wait_ge(s_at, atu(p) + UH + (4 if q == 0 else UH))
                for b in range(QB):
                    cols = slice(b * P, (b + 1) * P)
                    for k, (t, w) in enumerate(parts):
                        block_b = t[:, ds(q * QN + b * P, P)]
                        if w is None:
                            last = t_.transpose(y[:, cols], block_b, ident[:, :])
                        else:
                            last = t_.matmul(y[:, cols], block_b, w, start=k == 0, stop=k == len(parts) - 1)
                last.then_inc(s_yf, 1)

            def turn(p, q, source):
                pe.wait_ge(s_zfree, ZU[p] + q + 1)
                for b in range(QB):
                    last = t_.transpose(Z[:, b * P:(b + 1) * P], source[:, ds(q * QN + b * P, P)], ident[:, :])
                last.then_inc(s_zf, 1)

            def edge_group(g, k):
                pe.wait_ge(s_ahl, g + 1)
                if not (isinstance(g, int) and g == 0):
                    pe.wait_ge(s_eae, g + 1)
                for j in range(J):
                    last = mm(CH[:, 0:WIN], AHL[k][:, j, :], OHW[k][:, j, :], start=j == 0)
                last.then_inc(s_eam, 1)

            def fast(p):
                slot = ring(p)
                pe.wait_ge(s_tb, TU[p - 1] + 7)
                for h in range(2):
                    n = 2 * (p - 1) + h

                    def block_(k, m, use, first=False):
                        pe.wait_ge(s_al[m], 16 * use)
                        cols = ds(k * P, P) if not isinstance(k, int) else slice(k * P, k * P + P)
                        for part in (HI, LO):
                            for j in range(UH):
                                if first and part is HI and h:
                                    pe.wait_ge(s_at, atu(p) + j + 1)
                                last = mm(AGB[j], part[:, cols], slot[m][:, UN * j:UN * (j + 1)], start=first and part is HI)
                        last.then_inc(s_af[m], 1)

                    def four(i, edges=None):
                        for m in range(RING):
                            block_(RING * i + 1 + m, m, 12 * n + i + 1)
                            if edges and edges[m]:
                                edge_group(*edges[m])

                    if h == 0:
                        pe.wait_ge(s_split, 7 * p + 1)
                    block_(0, RING, n + 1, True)
                    steps = (NB - 1) // RING

                    def with_edges(i0, i1, g):
                        with pe.Fori(i0, i1) as i:
                            first_ = 6 * i + (g - 6 * i0)
                            four(2 * i, [None, (first_, 1), (first_ + 1, 0), (first_ + 2, 1)])
                            four(2 * i + 1, [None, (first_ + 3, 0), (first_ + 4, 1), (first_ + 5, 0)])

                    if h == 0:
                        with pe.Fori(0, NQ) as i:
                            pe.wait_ge(s_split, i + 7 * p + 1)
                            four(i)
                        if p == 4:
                            four(NQ)
                            measured(EDGES)
                            edge_group(0, 0)
                            with_edges((NQ + 1) // 2, steps // 2, 1)
                        else:
                            with pe.Fori(NQ, steps) as i:
                                four(i)
                    elif p == 4:
                        with_edges(0, steps // 2, 13)
                    else:
                        with pe.Fori(0, steps) as i:
                            four(i)
                    if p in SELF:
                        for j in range(UH):
                            for blk_, c0, d0, w_ in ahead(UH * h + j):
                                for part in (HI, LO):
                                    mm(AGB[j][:, d0:d0 + w_], part[:, blk_ * P:(blk_ + 1) * P], I16[:, c0:c0 + w_])
                    pe.drain().then_inc(s_agg, 1)

            with pe.If(flags["pe"]):
                pe.wait_ge(s_at, NU)
                general("cnt")
                general("attr")
                general(0)
                sums(agu(0), 1)
                pe.wait_ge(s_at0, NQ)
            for p in range(8):
                if p:
                    with pe.If(flags["pe"]):
                        general(p)
                        if p == 4:
                            sums(agu(4) - 7, 5)
                        sums(agu(p), p + 1 + (p >= 4))
                        pe.wait_ge(s_at, atu(p + 1))
                    with pe.Else():
                        fast(p)
                if p == 0:
                    pe.wait_ge(s_at, atu(1))
                if p in (0, 1):
                    w = WT[:, 0, :] if p == 0 else WN[:, 0, :]

                    def hidden(q):
                        pe.wait_ge(s_xfree, XU[p] + q + 1)
                        if q < 4 and p:
                            pe.wait_ge(s_at, atu(p) + max(UH + 2, 2 * q + 2))
                        for h in range(2):
                            last = t_.matmul(X[:, 512 * h:512 * h + UN], w, AT[:, ds(q * QN + h * UN, UN)], start=True, stop=True)
                        last.then_inc(s_xf, 1)

                    hidden(0)
                    for q in range(NQ):
                        if q + 1 < NQ:
                            hidden(q + 1)
                        pe.wait_ge(s_tb, TU[p] + q + 1)
                        node_stage(p, YU[p], q, [(TB, WT[:, 1, :] if p == 0 else WN[:, 1, :])])
                elif p in (2, 3):
                    for q in range(NQ):
                        pe.wait_ge(s_tb, TU[p] + q + 1)
                        node_stage(p, YU[p], q, [(TB, WN[:, p, :])])
                elif p == 4:
                    def layer_2(q):
                        pe.wait_ge(s_tb, TU[p] + q + 1)
                        pe.wait_ge(s_xfree, XU[p] + q + 1)
                        for b in range(QB):
                            last = t_.matmul(X[:, b * P:(b + 1) * P], TB[:, ds(q * QN + b * P, P)], WN[:, 4, :], start=True, stop=True)
                        last.then_inc(s_xf, 1)

                    for q in range(NQ + 3):
                        if q < NQ:
                            node_stage(p, YU[p], q, [(AT, None)])
                        if 2 <= q < NQ + 2:
                            if q == 2:
                                pe.wait_ge(s_at, atu(p + 1))
                            pe.wait_ge(s_xn, q - 1)
                            turn(p, q - 2, XN)
                        if q >= 3:
                            layer_2(q - 3)
                elif p == 5:
                    for q in range(NQ):
                        node_stage(p, YU[p], q, [(AT, ident[:, :]), (RB, We2[:, :])])
                        if q >= 2:
                            pe.wait_ge(s_xn, 7 + q - 1)
                            turn(p, q - 2, XN)
                    for q in (NQ - 2, NQ - 1):
                        pe.wait_ge(s_xn, 7 + q + 1)
                        turn(p, q, XN)
                elif p == 6:
                    for q in range(NQ):
                        node_stage(p, YU[p], q, [(AT, WT[:, 2, :]), (TB, WT[:, 3, :])])
                        if q:
                            pe.wait_ge(s_h, 7 * 6 + q)
                            turn(p, q - 1, HN)
                    pe.wait_ge(s_h, 7 * 6 + NQ)
                    turn(p, NQ - 1, HN)
                else:
                    pe.wait_ge(s_tb, TU[6] + 7)
                    for q in range(NQ):
                        node_stage(p, YU[p], q, [(AT, WT[:, 4, :]), (TB, WT[:, 5, :])])
                if p + 1 in MEASURED:
                    measured(p + 1)


_INS = ['x', 'src', 'dst', 'edge_attr_64', 'L0_gnn_W1', 'L0_gnn_b1', 'L0_gnn_W2', 'L0_gnn_b2', 'L1_gnn_W1', 'L1_gnn_b1',
        'L1_gnn_W2', 'L1_gnn_b2', 'L1_gnn_W3', 'L1_gnn_b3', 'L1_gnn_W4', 'L1_gnn_b4', 'L2_gnn_Wn', 'L2_gnn_bn',
        'L2_gnn_We', 'L2_gnn_be', 'L2_gnn_resid', 'L3_gnn_W_l0', 'L3_gnn_b_l0', 'L3_gnn_W_r0', 'L3_gnn_W_l1',
        'L3_gnn_b_l1', 'L3_gnn_W_r1']


def kernel(**inputs):
    import numpy as _np
    import concourse.bacc as _bacc
    from concourse import mybir as _mybir
    from concourse.bass_utils import run_bass_kernel_spmd as _run

    nc = _bacc.Bacc("TRN2", target_bir_lowering=False, num_devices=1)
    arrays, aps = {}, {}
    for name in _INS:
        v = _np.ascontiguousarray(inputs[name])
        arrays[f"in_{name}_dram"] = v
        aps[name] = nc.dram_tensor(f"in_{name}_dram", v.shape, _mybir.dt.from_np(v.dtype), kind="ExternalInput").ap()
    out = nc.dram_tensor("out_0_dram", inputs["x"].shape, _mybir.dt.float32, kind="ExternalOutput").ap()
    build(nc, aps, out)
    r = _run(nc, [arrays], core_ids=[0])
    return r.results[0]["out_0_dram"]
```
